# Optimizing a Trainium2 kernel written in Bass

```python
import numpy as np
import jax
import jax.numpy as jnp

def _softmax(x, axis=-1):
    return jax.nn.softmax(x, axis=axis)

def _gelu(x):
    return jax.nn.gelu(x, approximate=True)

def _silu(x):
    return jax.nn.silu(x)

def _sigmoid(x):
    return jax.nn.sigmoid(x)

def _layernorm(x, axis=-1, eps=1e-05):
    m = jnp.mean(x, axis=axis, keepdims=True)
    v = jnp.var(x, axis=axis, keepdims=True)
    return (x - m) / jnp.sqrt(v + eps)

def _scatter_add(tgt, idx, src, axis=0):
    return tgt.at[idx].add(src)

def _segment_sum(src, seg, n):
    return jax.ops.segment_sum(src, seg, n)
kernel_name = 'mk_lm_tower_d1_tok_ids256_r4_4ba8a2'

def setup_inputs(seed: int=0):
    np.random.seed(seed)
    _w = jnp.asarray

    def _rec_inputs():
        import jax
        import jax.numpy as jnp
        _rk = jax.random.key(seed)
        x = jax.random.randint(jax.random.fold_in(_rk, 1), (4, 512), 0, 64, jnp.int32)
        fside_BS_continuous_positions = jax.random.uniform(jax.random.fold_in(_rk, 21), (4, 512), jnp.float32, 0.0, 0.999927)
        return (x, fside_BS_continuous_positions)
    x, fside_BS_continuous_positions = _rec_inputs()

    def _L0_tok_setup():
        import jax, jax.numpy as jnp
        import numpy as np
        N_SCALES = 4

        def _conv1d(x, w, b, pad):
            y = jax.lax.conv_general_dilated(x, w, window_strides=(1,), padding=[(pad, pad)], dimension_numbers=('NCH', 'OIH', 'NCH'))
            return y + b[None, :, None]
        key = jax.random.key(seed)
        ks = jax.random.split(key, 12)
        B, S, P, D = (8, 512, 512, 64)
        byte_sequence = jax.random.randint(ks[0], (B, S), 0, 64, dtype=jnp.int64)
        continuous_positions = jax.random.uniform(ks[1], (B, P), dtype=jnp.float32)
        emb = jax.random.normal(ks[2], (64, D), dtype=jnp.float32)
        locality_shapes = jax.random.normal(ks[3], (64, 4), dtype=jnp.float32)
        w1 = jax.random.normal(ks[4], (128, 64, 7), dtype=jnp.float32) * 0.02
        b1 = jnp.zeros((128,), dtype=jnp.float32)
        w2 = jax.random.normal(ks[5], (64, 128, 5), dtype=jnp.float32) * 0.02
        b2 = jnp.zeros((64,), dtype=jnp.float32)
        w3 = jax.random.normal(ks[6], (1, 64, 3), dtype=jnp.float32) * 0.02
        b3 = jnp.zeros((1,), dtype=jnp.float32)
        multiscale_widths = jnp.array([0.01, 0.02, 0.05, 0.1], dtype=jnp.float32)
        scale_weights = jnp.ones((4,), dtype=jnp.float32)
        return {'byte_sequence': byte_sequence, 'continuous_positions': continuous_positions, 'emb': emb, 'locality_shapes': locality_shapes, 'w1': w1, 'b1': b1, 'w2': w2, 'b2': b2, 'w3': w3, 'b3': b3, 'multiscale_widths': multiscale_widths, 'scale_weights': scale_weights}
    _L0_tok_all = _L0_tok_setup()
    _L0_tok_in = {k: v for k, v in _L0_tok_all.items() if k in ('emb', 'locality_shapes', 'w1', 'b1', 'w2', 'b2', 'w3', 'b3', 'multiscale_widths', 'scale_weights')}
    del _L0_tok_all

    def _L0_attn_setup():
        import jax, jax.numpy as jnp
        import numpy as np
        B_, L_, D_ = (4, 1024, 64)
        EXPAND = 2
        DI_ = EXPAND * D_
        H_ = 8
        P_ = DI_ // H_
        N_ = 16
        K_ = 3

        def _layernorm(x, w, b):
            m = x.mean(-1, keepdims=True)
            v = ((x - m) ** 2).mean(-1, keepdims=True)
            return (x - m) * jax.lax.rsqrt(v + 1e-05) * w + b

        def _mh_ssm(x, in_w, in_b, xp_w, xp_b, dt_b, A_log, D_skip, out_w, out_b):
            Bsz, L, _ = x.shape
            xz = x @ in_w.T + in_b
            xi, z = jnp.split(xz, 2, axis=-1)
            xi = jax.nn.silu(xi)
            proj = xi @ xp_w.T + xp_b
            dt = jax.nn.softplus(proj[..., :DI_] + dt_b)
            Bm = proj[..., DI_:DI_ + H_ * N_].reshape(Bsz, L, H_, N_)
            Cm = proj[..., DI_ + H_ * N_:].reshape(Bsz, L, H_, N_)
            A = -jnp.exp(A_log).reshape(H_, P_, N_)
            x4 = xi.reshape(Bsz, L, H_, P_)
            dt4 = dt.reshape(Bsz, L, H_, P_)

            def step(h, t):
                xt, dtt, Bt, Ct = t
                dA = jnp.exp(dtt[..., None] * A)
                h = h * dA + dtt[..., None] * Bt[:, :, None, :] * xt[..., None]
                y = jnp.einsum('bhpn,bhn->bhp', h, Ct)
                return (h, y)
            xs = (x4.transpose(1, 0, 2, 3), dt4.transpose(1, 0, 2, 3), Bm.transpose(1, 0, 2, 3), Cm.transpose(1, 0, 2, 3))
            h0 = jnp.zeros((Bsz, H_, P_, N_), x.dtype)
            _, ys = jax.lax.scan(step, h0, xs)
            y = ys.transpose(1, 0, 2, 3).reshape(Bsz, L, DI_) + xi * D_skip
            y = y * jax.nn.silu(z)
            return y @ out_w.T + out_b
        key = jax.random.key(seed)
        ks = jax.random.split(key, 32)

        def n(i, shape, s=0.02):
            return jax.random.normal(ks[i], shape, jnp.float32) * s
        inp = {'inputs': jax.random.normal(ks[0], (B_, L_, D_), jnp.float32)}
        i = 1
        for pre in ('f_', 'b_'):
            inp[pre + 'in_proj_w'] = n(i, (2 * DI_, D_))
            i += 1
            inp[pre + 'in_proj_b'] = jnp.zeros((2 * DI_,), jnp.float32)
            inp[pre + 'x_proj_w'] = n(i, (DI_ + 2 * H_ * N_, DI_))
            i += 1
            inp[pre + 'x_proj_b'] = jnp.zeros((DI_ + 2 * H_ * N_,), jnp.float32)
            inp[pre + 'dt_bias'] = jnp.full((DI_,), -4.0, jnp.float32)
            inp[pre + 'A_log'] = jnp.log(jnp.tile(jnp.arange(1, N_ + 1, dtype=jnp.float32), (DI_, 1)))
            inp[pre + 'D_skip'] = jnp.ones((DI_,), jnp.float32)
            inp[pre + 'out_proj_w'] = n(i, (D_, DI_))
            i += 1
            inp[pre + 'out_proj_b'] = jnp.zeros((D_,), jnp.float32)
        inp['norm_w'] = jnp.ones((D_,), jnp.float32)
        inp['norm_b'] = jnp.zeros((D_,), jnp.float32)
        inp['conv_w'] = n(20, (D_, 1, K_), 0.1)
        inp['conv_b'] = jnp.zeros((D_,), jnp.float32)
        return inp
    _L0_attn_all = _L0_attn_setup()
    _L0_attn_in = {k: v for k, v in _L0_attn_all.items() if k in ('f_in_proj_w', 'f_in_proj_b', 'f_x_proj_w', 'f_x_proj_b', 'f_dt_bias', 'f_A_log', 'f_D_skip', 'f_out_proj_w', 'f_out_proj_b', 'b_in_proj_w', 'b_in_proj_b', 'b_x_proj_w', 'b_x_proj_b', 'b_dt_bias', 'b_A_log', 'b_D_skip', 'b_out_proj_w', 'b_out_proj_b', 'norm_w', 'norm_b', 'conv_w', 'conv_b')}
    del _L0_attn_all

    def _L0_ffn_setup():
        import jax, jax.numpy as jnp
        import numpy as np
        B, S, D = (8, 1024, 64)
        H = 4 * D
        CAPACITY = 0.5
        key = jax.random.key(seed)
        ks = jax.random.split(key, 6)
        x = jax.random.normal(ks[0], (B, S, D), dtype=jnp.float32)
        attention_mask = jnp.zeros((B, 1, 1, S), dtype=jnp.float32)
        wr = jax.random.normal(ks[1], (D, 1), dtype=jnp.float32) * 0.02
        br = jnp.zeros((1,), dtype=jnp.float32)
        w1 = jax.random.normal(ks[2], (D, H), dtype=jnp.float32) * 0.02
        b1 = jnp.zeros((H,), dtype=jnp.float32)
        w2 = jax.random.normal(ks[3], (H, D), dtype=jnp.float32) * 0.02
        b2 = jnp.zeros((D,), dtype=jnp.float32)
        return {'x': x, 'attention_mask': attention_mask, 'wr': wr, 'br': br, 'w1': w1, 'b1': b1, 'w2': w2, 'b2': b2}
    _L0_ffn_all = _L0_ffn_setup()
    _L0_ffn_in = {k: v for k, v in _L0_ffn_all.items() if k in ('attention_mask', 'wr', 'br', 'w1', 'b1', 'w2', 'b2')}
    del _L0_ffn_all
    return {'x': x, 'fside_BS_continuous_positions': fside_BS_continuous_positions, 'L0_tok_emb': _L0_tok_in['emb'], 'L0_tok_locality_shapes': _L0_tok_in['locality_shapes'], 'L0_tok_w1': _L0_tok_in['w1'], 'L0_tok_b1': _L0_tok_in['b1'], 'L0_tok_w2': _L0_tok_in['w2'], 'L0_tok_b2': _L0_tok_in['b2'], 'L0_tok_w3': _L0_tok_in['w3'], 'L0_tok_b3': _L0_tok_in['b3'], 'L0_tok_multiscale_widths': _L0_tok_in['multiscale_widths'], 'L0_tok_scale_weights': _L0_tok_in['scale_weights'], 'L0_attn_f_in_proj_w': _L0_attn_in['f_in_proj_w'], 'L0_attn_f_in_proj_b': _L0_attn_in['f_in_proj_b'], 'L0_attn_f_x_proj_w': _L0_attn_in['f_x_proj_w'], 'L0_attn_f_x_proj_b': _L0_attn_in['f_x_proj_b'], 'L0_attn_f_dt_bias': _L0_attn_in['f_dt_bias'], 'L0_attn_f_A_log': _L0_attn_in['f_A_log'], 'L0_attn_f_D_skip': _L0_attn_in['f_D_skip'], 'L0_attn_f_out_proj_w': _L0_attn_in['f_out_proj_w'], 'L0_attn_f_out_proj_b': _L0_attn_in['f_out_proj_b'], 'L0_attn_b_in_proj_w': _L0_attn_in['b_in_proj_w'], 'L0_attn_b_in_proj_b': _L0_attn_in['b_in_proj_b'], 'L0_attn_b_x_proj_w': _L0_attn_in['b_x_proj_w'], 'L0_attn_b_x_proj_b': _L0_attn_in['b_x_proj_b'], 'L0_attn_b_dt_bias': _L0_attn_in['b_dt_bias'], 'L0_attn_b_A_log': _L0_attn_in['b_A_log'], 'L0_attn_b_D_skip': _L0_attn_in['b_D_skip'], 'L0_attn_b_out_proj_w': _L0_attn_in['b_out_proj_w'], 'L0_attn_b_out_proj_b': _L0_attn_in['b_out_proj_b'], 'L0_attn_norm_w': _L0_attn_in['norm_w'], 'L0_attn_norm_b': _L0_attn_in['norm_b'], 'L0_attn_conv_w': _L0_attn_in['conv_w'], 'L0_attn_conv_b': _L0_attn_in['conv_b'], 'L0_ffn_attention_mask': _L0_ffn_in['attention_mask'], 'L0_ffn_wr': _L0_ffn_in['wr'], 'L0_ffn_br': _L0_ffn_in['br'], 'L0_ffn_w1': _L0_ffn_in['w1'], 'L0_ffn_b1': _L0_ffn_in['b1'], 'L0_ffn_w2': _L0_ffn_in['w2'], 'L0_ffn_b2': _L0_ffn_in['b2']}

def reference(x, fside_BS_continuous_positions, L0_tok_emb, L0_tok_locality_shapes, L0_tok_w1, L0_tok_b1, L0_tok_w2, L0_tok_b2, L0_tok_w3, L0_tok_b3, L0_tok_multiscale_widths, L0_tok_scale_weights, L0_attn_f_in_proj_w, L0_attn_f_in_proj_b, L0_attn_f_x_proj_w, L0_attn_f_x_proj_b, L0_attn_f_dt_bias, L0_attn_f_A_log, L0_attn_f_D_skip, L0_attn_f_out_proj_w, L0_attn_f_out_proj_b, L0_attn_b_in_proj_w, L0_attn_b_in_proj_b, L0_attn_b_x_proj_w, L0_attn_b_x_proj_b, L0_attn_b_dt_bias, L0_attn_b_A_log, L0_attn_b_D_skip, L0_attn_b_out_proj_w, L0_attn_b_out_proj_b, L0_attn_norm_w, L0_attn_norm_b, L0_attn_conv_w, L0_attn_conv_b, L0_ffn_attention_mask, L0_ffn_wr, L0_ffn_br, L0_ffn_w1, L0_ffn_b1, L0_ffn_w2, L0_ffn_b2):
    import jax
    import jax.numpy as jnp

    def _L0_tok_ref(byte_sequence, continuous_positions, emb, locality_shapes, w1, b1, w2, b2, w3, b3, multiscale_widths, scale_weights):
        import jax, jax.numpy as jnp
        import numpy as np
        N_SCALES = 4

        def _conv1d(x, w, b, pad):
            y = jax.lax.conv_general_dilated(x, w, window_strides=(1,), padding=[(pad, pad)], dimension_numbers=('NCH', 'OIH', 'NCH'))
            return y + b[None, :, None]
        B, S = byte_sequence.shape
        P = continuous_positions.shape[1]
        amps = emb[byte_sequence]
        onehot = jax.nn.one_hot(byte_sequence, 64, dtype=jnp.float32)
        onehot = jnp.transpose(onehot, (0, 2, 1))
        h = jax.nn.gelu(_conv1d(onehot, w1, b1, 3), approximate=False)
        h = jax.nn.gelu(_conv1d(h, w2, b2, 2), approximate=False)
        ctx = jax.nn.sigmoid(_conv1d(h, w3, b3, 1))[:, 0, :]
        amps = amps * ctx[:, :, None]
        lp = locality_shapes[byte_sequence]
        byte_pos = jnp.linspace(0.0, 1.0, S, dtype=jnp.float32)
        center = byte_pos[None, :] + lp[..., 0] * 0.05
        xd = continuous_positions[:, None, :] - center[..., None]
        amp_scale = jax.nn.sigmoid(lp[..., 2])
        phase = lp[..., 3] * jnp.pi
        abs_w = jnp.abs(lp[..., 1])
        TWO_PI = 2.0 * jnp.pi
        basis_total = jnp.zeros((B, S, P), dtype=jnp.float32)
        for s in range(N_SCALES):
            width = abs_w * multiscale_widths[s] + 1e-05
            z = xd / width[..., None]
            basis = jnp.exp(-0.5 * z * z) * jnp.cos(phase[..., None] + TWO_PI * z)
            basis_total = basis_total + basis * (amp_scale[..., None] * scale_weights[s] ** 2)
        semantic_field = jnp.einsum('bsp,bsd->bpd', basis_total, amps)
        return semantic_field

    def _L0_attn_ref(inputs, f_in_proj_w, f_in_proj_b, f_x_proj_w, f_x_proj_b, f_dt_bias, f_A_log, f_D_skip, f_out_proj_w, f_out_proj_b, b_in_proj_w, b_in_proj_b, b_x_proj_w, b_x_proj_b, b_dt_bias, b_A_log, b_D_skip, b_out_proj_w, b_out_proj_b, norm_w, norm_b, conv_w, conv_b):
        import jax, jax.numpy as jnp
        import numpy as np
        B_, L_, D_ = (4, 1024, 64)
        EXPAND = 2
        DI_ = EXPAND * D_
        H_ = 8
        P_ = DI_ // H_
        N_ = 16
        K_ = 3

        def _layernorm(x, w, b):
            m = x.mean(-1, keepdims=True)
            v = ((x - m) ** 2).mean(-1, keepdims=True)
            return (x - m) * jax.lax.rsqrt(v + 1e-05) * w + b

        def _mh_ssm(x, in_w, in_b, xp_w, xp_b, dt_b, A_log, D_skip, out_w, out_b):
            Bsz, L, _ = x.shape
            xz = x @ in_w.T + in_b
            xi, z = jnp.split(xz, 2, axis=-1)
            xi = jax.nn.silu(xi)
            proj = xi @ xp_w.T + xp_b
            dt = jax.nn.softplus(proj[..., :DI_] + dt_b)
            Bm = proj[..., DI_:DI_ + H_ * N_].reshape(Bsz, L, H_, N_)
            Cm = proj[..., DI_ + H_ * N_:].reshape(Bsz, L, H_, N_)
            A = -jnp.exp(A_log).reshape(H_, P_, N_)
            x4 = xi.reshape(Bsz, L, H_, P_)
            dt4 = dt.reshape(Bsz, L, H_, P_)

            def step(h, t):
                xt, dtt, Bt, Ct = t
                dA = jnp.exp(dtt[..., None] * A)
                h = h * dA + dtt[..., None] * Bt[:, :, None, :] * xt[..., None]
                y = jnp.einsum('bhpn,bhn->bhp', h, Ct)
                return (h, y)
            xs = (x4.transpose(1, 0, 2, 3), dt4.transpose(1, 0, 2, 3), Bm.transpose(1, 0, 2, 3), Cm.transpose(1, 0, 2, 3))
            h0 = jnp.zeros((Bsz, H_, P_, N_), x.dtype)
            _, ys = jax.lax.scan(step, h0, xs)
            y = ys.transpose(1, 0, 2, 3).reshape(Bsz, L, DI_) + xi * D_skip
            y = y * jax.nn.silu(z)
            return y @ out_w.T + out_b
        y1 = _mh_ssm(inputs, f_in_proj_w, f_in_proj_b, f_x_proj_w, f_x_proj_b, f_dt_bias, f_A_log, f_D_skip, f_out_proj_w, f_out_proj_b)
        y1n = jnp.flip(_layernorm(y1, norm_w, norm_b), axis=1)
        y2 = _mh_ssm(y1n, b_in_proj_w, b_in_proj_b, b_x_proj_w, b_x_proj_b, b_dt_bias, b_A_log, b_D_skip, b_out_proj_w, b_out_proj_b)
        out = jnp.flip(y2, axis=1)
        xt = inputs.transpose(0, 2, 1)
        c = jax.lax.conv_general_dilated(xt, conv_w, window_strides=(1,), padding=[(1, 1)], dimension_numbers=('NCH', 'OIH', 'NCH'), feature_group_count=D_)
        c = jax.nn.gelu(c + conv_b[None, :, None], approximate=False)
        return out + c.transpose(0, 2, 1)

    def _L0_ffn_ref(x, attention_mask, wr, br, w1, b1, w2, b2):
        import jax, jax.numpy as jnp
        import numpy as np
        B, S, D = (8, 1024, 64)
        H = 4 * D
        CAPACITY = 0.5
        b, s, d = x.shape
        weights = (jnp.einsum('bsd,do->bso', x, wr) + br)[..., 0]
        k = max(1, int(CAPACITY * s))
        kk = k - 1 if k > 1 else 1
        _, idx = jax.lax.top_k(weights, k)
        sel_idx = idx[:, :kk]
        sel = jnp.take_along_axis(x, sel_idx[:, :, None], axis=1)
        h = jax.nn.gelu(jnp.einsum('bkd,dh->bkh', sel, w1) + b1)
        y = jnp.einsum('bkh,hd->bkd', h, w2) + b2
        w_sel = jnp.take_along_axis(weights, sel_idx, axis=1)
        y = y * w_sel[..., None]
        batch_idx = jnp.arange(b)[:, None]
        processed = jnp.zeros_like(x).at[batch_idx, sel_idx].set(y)
        return processed + x
    h = _L0_tok_ref(x, fside_BS_continuous_positions, L0_tok_emb, L0_tok_locality_shapes, L0_tok_w1, L0_tok_b1, L0_tok_w2, L0_tok_b2, L0_tok_w3, L0_tok_b3, L0_tok_multiscale_widths, L0_tok_scale_weights)
    h = h + _L0_attn_ref(_layernorm(h, axis=-1), L0_attn_f_in_proj_w, L0_attn_f_in_proj_b, L0_attn_f_x_proj_w, L0_attn_f_x_proj_b, L0_attn_f_dt_bias, L0_attn_f_A_log, L0_attn_f_D_skip, L0_attn_f_out_proj_w, L0_attn_f_out_proj_b, L0_attn_b_in_proj_w, L0_attn_b_in_proj_b, L0_attn_b_x_proj_w, L0_attn_b_x_proj_b, L0_attn_b_dt_bias, L0_attn_b_A_log, L0_attn_b_D_skip, L0_attn_b_out_proj_w, L0_attn_b_out_proj_b, L0_attn_norm_w, L0_attn_norm_b, L0_attn_conv_w, L0_attn_conv_b)
    h = h + _L0_ffn_ref(_layernorm(h, axis=-1), L0_ffn_attention_mask, L0_ffn_wr, L0_ffn_br, L0_ffn_w1, L0_ffn_b1, L0_ffn_w2, L0_ffn_b2)
    return h

_drawn_inputs = setup_inputs


def setup_inputs(seed=0):
    import zlib

    import numpy as np

    out = dict(_drawn_inputs(seed))
    spreads = {'L0_tok_b1': (0.0, 0.8),
     'L0_tok_b2': (0.0, 0.8),
     'L0_tok_scale_weights': (1.0, 0.2),
     'L0_attn_f_in_proj_b': (0.0, 0.8),
     'L0_attn_f_x_proj_b': (0.0, 0.8),
     'L0_attn_f_dt_bias': (-4.0, 0.6),
     'L0_attn_f_D_skip': (1.0, 0.6),
     'L0_attn_f_out_proj_b': (0.0, 0.8),
     'L0_attn_b_in_proj_b': (0.0, 0.8),
     'L0_attn_b_x_proj_b': (0.0, 0.8),
     'L0_attn_b_dt_bias': (-4.0, 0.6),
     'L0_attn_b_D_skip': (1.0, 0.6),
     'L0_attn_b_out_proj_b': (0.0, 2.0),
     'L0_attn_norm_w': (1.0, 0.6),
     'L0_attn_norm_b': (0.0, 0.8),
     'L0_attn_conv_b': (0.0, 2.0),
     'L0_ffn_b1': (0.0, 2.0),
     'L0_ffn_b2': (0.0, 2.0)}
    factors = {'L0_tok_w1': 8.0,
     'L0_tok_w2': 8.0,
     'L0_tok_w3': 8.0,
     'L0_attn_f_in_proj_w': 8.0,
     'L0_attn_f_x_proj_w': 8.0,
     'L0_attn_f_A_log': 8.0,
     'L0_attn_f_out_proj_w': 8.0,
     'L0_attn_b_in_proj_w': 8.0,
     'L0_attn_b_x_proj_w': 8.0,
     'L0_attn_b_A_log': 8.0,
     'L0_attn_b_out_proj_w': 8.0,
     'L0_ffn_wr': 8.0,
     'L0_ffn_w1': 8.0,
     'L0_ffn_w2': 8.0,
     'L0_attn_conv_w': 33.74}
    for name, (base, spread) in spreads.items():
        noise = np.random.default_rng([zlib.crc32(name.encode()), seed]).standard_normal(out[name].shape)
        drawn = base * np.exp(spread * noise) if base else spread * noise
        out[name] = jnp.asarray(drawn.astype(out[name].dtype))
    for name, factor in factors.items():
        out[name] = (out[name] * factor).astype(out[name].dtype)
    return out
```

```python
from contextlib import ExitStack

import numpy as np

import concourse.bass as bass
from concourse import mybir

ALU = mybir.AluOpType
ACT = mybir.ActivationFunctionType
F32 = mybir.dt.float32
BF16 = mybir.dt.bfloat16
I32 = mybir.dt.int32

BATCH, SEQ, D = 4, 512, 64
VOCAB = 64
HID = 128
K1, K2, K3 = 7, 5, 3
KD = 3
SCALES = 4
ST = SEQ // 128
TILES = BATCH * ST
DI, HEADS, P_DIM, N_DIM = 128, 8, 16, 16
G = 4
PL = P_DIM // G
FF = 256
CAP = SEQ // 2 - 1
UNITS = 2 * BATCH
LN_EPS = 1e-5
ROUND = 1.5 * 2.0 ** 23
TWO_PI = 6.283185

RB = 6
RX = 4
RC = 4
LAG = 3


def columns(parts):
    at, out = 0, {}
    for name, n in parts:
        out[name] = (at, at + n)
        at += n
    return out, at


W128, W128_N = columns(
    [("tok_w2", K2 * D), ("tok_b1", 1), ("b3", 1), ("widths", SCALES), ("sw", SCALES), ("br", 1),
     ("ffn_w2", 2 * D), ("ffn_b1", 2)]
    + [(f"{d}_{n}", k) for d in "fb" for n, k in
       (("xp_dt", DI), ("xp_B", DI), ("xp_C", DI), ("in_bx", 1), ("in_bz", 1), ("xp_bdt", 1), ("dt_bias", 1),
        ("xp_bB", 1), ("xp_bC", 1), ("D_skip", 1), ("A_log", P_DIM), ("out_w", D))])
W64, W64_N = columns(
    [("embloc", D + 4), ("tok_w1", K1 * HID), ("w3", K3), ("b2", 1), ("norm_w", 1), ("norm_b", 1),
     ("conv_w", KD), ("conv_b", 1), ("ffn_w1", FF), ("wr", 128), ("ffn_b2", 1)]
    + [(f"{d}_{n}", k) for d in "fb" for n, k in (("in_wx", DI), ("in_wz", DI), ("out_b", 1))])
C128, C128_N = columns(
    [("sel", PL * 128), ("ssum", PL * 32), ("tri", 128), ("place", TILES), ("eps", 1), ("one", 1), ("mean", D),
     ("vocab", 1)])


def make_plan():
    plan = {}

    def add(u, slot, name, v):
        plan.setdefault((u, slot), []).append((name, v))

    def front(v, u, s):
        if v < BATCH:
            for k, n in enumerate(("ln1_mean", "ln1_center", "ln1_square", "ln1_var", "ln1_rstd", "ln1_out")):
                add(u, s + k, n, v)
        s += 6
        for k, n in enumerate(("in_proj", "silu", "x_proj", "softplus", "x_proj_C", "dt")):
            add(u, s + k, n, v)

    def post(v, u, s):
        names = ["gate", "out_proj"]
        if v < BATCH:
            names += ["out_bias", "ln2_mean", "ln2_center", "ln2_square", "ln2_var", "ln2_rstd", "ln2_scale", "ln2_out"]
        else:
            names += ["h2", "ln3_mean", "ln3_center", "ln3_square", "ln3_var", "ln3_rstd", "ln3_out"]
        for k, n in enumerate(names):
            add(u, s + k, n, v)

    def ffn(v, u, s):
        for k, n in ((0, "ffn_route"), (1, "ffn_route_copy"), (2, "ffn_col"), (3, "ffn_col_copy"), (3, "ffn_rank"),
                     (4, "ffn_rank_sum"), (5, "ffn_mask"), (12, "ffn_up"), (13, "ffn_gelu"), (14, "ffn_down"),
                     (15, "ffn_out")):
            add(u, s + k, n, v)

    front(0, -1, 0)
    for v in range(UNITS):
        if v + 1 < UNITS:
            front(v + 1, v, 0)
        if v >= 1:
            post(v - 1, v, 4)
        if v - 2 >= BATCH:
            ffn(v - 2, v, 0)
        if v == BATCH - 1:
            for b in range(BATCH):
                add(v, 13, "conv_gelu", b)
    for b in range(BATCH):
        add(b, 12, "conv", b)
    post(UNITS - 1, UNITS, 0)
    ffn(UNITS - 2, UNITS, 0)
    ffn(UNITS - 1, UNITS, 11)
    slots = [(-1, s) for s in range(16)] + [(u, s) for u in range(UNITS) for s in range(P_DIM)]
    slots += [(UNITS, s) for s in range(32)]
    return plan, slots


PLAN, SLOTS = make_plan()
SHARED_FILLS = {"ln1_mean": ["m1"], "ln1_var": ["v1"], "in_proj": ["xi", "z"], "x_proj": ["dt", "B"],
                "x_proj_C": ["C"], "out_proj": ["o"], "ln2_mean": ["m2"], "ln2_var": ["v2"], "ln3_mean": ["m3"],
                "ln3_var": ["v3"], "ffn_route": ["w"], "ffn_col": ["wc"], "ffn_rank_sum": ["rank"],
                "ffn_up": ["up0", "up1"], "ffn_down": ["y"]}


def number_fills():
    out, k = {}, 0
    for slot in SLOTS:
        for name, v in PLAN.get(slot, []):
            for product in SHARED_FILLS.get(name, []):
                out[product, v] = k
                k += 1
    return out


FILL = number_fills()


def build(nc, ids, w64, w128, pos, const, out):
    with ExitStack() as ctx:
        def sb(name, shape, dt=F32):
            return ctx.enter_context(nc.sbuf_tensor(name, shape, dt))

        def sem(name):
            return ctx.enter_context(nc.semaphore(name))

        bank = [ctx.enter_context(nc.psum_tensor(f"bank{i}", [128, 512], F32)) for i in range(8)]
        gathered, ctx_logit, conv1_ps, conv2_ps, field_ps = bank[0:3], bank[3], bank[4:6], bank[6:8], bank[0:2]
        dt_rep, dx_rep, y_ps, shared = bank[0:2], bank[2:4], bank[4:6], bank[6:8]

        ids_sb = sb("ids_sb", [VOCAB, BATCH, SEQ], I32)
        w64_sb = sb("w64_sb", [64, W64_N])
        w128_sb = sb("w128_sb", [128, W128_N])
        const_sb = sb("const_sb", [128, C128_N])
        pos_sb = sb("pos_sb", [128, BATCH, SEQ])

        def w64c(name, k=None):
            a, b = W64[name]
            return w64_sb[:, a:b] if k is None else w64_sb[:, a + k:a + k + 1]

        def w128c(name, k=None):
            a, b = W128[name]
            return w128_sb[:, a:b] if k is None else w128_sb[:, a + k:a + k + 1]

        def constc(name):
            a, b = C128[name]
            return const_sb[:, a:b]

        tok_w1 = w64c("tok_w1").rearrange("c (k o) -> c k o", k=K1)
        tok_w2 = w128c("tok_w2").rearrange("c (k o) -> c k o", k=K2)
        sel = constc("sel").rearrange("r (l n) -> r l n", l=PL)
        ssum = constc("ssum").rearrange("r (l n) -> r l n", l=PL)
        mean64 = constc("mean")[0:D, :]

        hot_all = sb("hot_all", [128, BATCH, SEQ + K1 - 1])
        hot = hot_all[0:VOCAB, :, :]
        loc = sb("loc", [128, TILES, D + 4])
        center = sb("center", [128, TILES])
        absw = sb("absw", [128, TILES])
        phase = sb("phase", [128, TILES])
        width = sb("width", [128, TILES, SCALES])
        inv_w = sb("inv_w", [128, TILES, SCALES])
        neg_half = sb("neg_half", [128, TILES, SCALES])
        amp_exp = sb("amp_exp", [128, TILES])
        amp_den = sb("amp_den", [128, TILES])
        amp_scale = sb("amp_scale", [128, TILES])
        sw2 = sb("sw2", [128, SCALES])
        scale_w = sb("scale_w", [128, TILES, SCALES])
        neg_b3 = sb("neg_b3", [128, 1])
        ctx_exp = sb("ctx_exp", [128, TILES])
        ctx_den = sb("ctx_den", [128, TILES])
        ctx_sig = sb("ctx_sig", [128, TILES])
        ctx_w = sb("ctx_w", [128, TILES, SCALES])
        amps = sb("amps", [128, TILES, SCALES, D])
        hid1 = sb("hid1", [HID, 2, SEQ + K2 - 1])
        hid2 = sb("hid2", [D, 2, SEQ + K3 - 1])
        xd = sb("xd", [128, RX, SEQ])
        xd2 = sb("xd2", [128, 2, SEQ])
        nearest = sb("nearest", [128, SCALES, SEQ])
        turn = sb("turn", [128, RB, SCALES, SEQ])
        env = sb("env", [128, RB, SCALES, SEQ])

        h1 = sb("h1", [D, BATCH, SEQ])
        xn = sb("xn", [D, BATCH, SEQ + 2])
        y1n = ids_sb[:, :, :].bitcast(F32)

        s_load = [sem(f"s_load{i}") for i in range(5)]
        s_hot = sem("s_hot")
        s_pad = sem("s_pad")
        s_gather = sem("s_gather")
        s_ampexp = sem("s_ampexp")
        s_param = sem("s_param")
        s_wgt = sem("s_wgt")
        s_conv1 = sem("s_conv1")
        s_hid1 = sem("s_hid1")
        s_conv2 = sem("s_conv2")
        s_hid2 = sem("s_hid2")
        s_conv3 = sem("s_conv3")
        s_negb3 = sem("s_negb3")
        s_ctxexp = sem("s_ctxexp")
        s_amps = sem("s_amps")
        s_xd = sem("s_xd")
        s_xd2 = sem("s_xd2")
        s_turn = sem("s_turn")
        s_env = sem("s_env")
        s_sin = sem("s_sin")
        s_wave = sem("s_wave")
        s_field = sem("s_field")
        s_fielddone = sem("s_fielddone")
        s_h1 = sem("s_h1")
        s_dve = sem("s_dve")
        s_act = sem("s_act")
        s_pool = sem("s_pool")
        s_fill = [sem("s_fill0"), sem("s_fill1")]
        s_evac = [sem("s_evac0"), sem("s_evac1")]

        def filled(eng, product, v):
            eng.wait_ge(s_fill[FILL[product, v] % 2], FILL[product, v] // 2 + 1)

        def evacuated(eng, product, v):
            eng.wait_ge(s_evac[FILL[product, v] % 2], FILL[product, v] // 2 + 1)

        names = "sq1 rstd1 xn sp_parts dt dtx gate sq2 rstd2 sc2 y1n conv cgelu sq3 rstd3 xn3 rankbits out bias A".split()
        S = {n: sem("s_" + n) for n in names}
        s_outdma = [sem("s_outdma0"), sem("s_outdma1")]
        s_dtrep = sem("s_dtrep")
        s_dxrep = sem("s_dxrep")
        s_decay = sem("s_decay")
        s_drive = sem("s_drive")
        s_state = sem("s_state")
        s_hc = sem("s_hc")
        s_ysum = sem("s_ysum")

        arena = [turn[:, i, :, :].rearrange("p s t -> p (s t)") for i in range(RB)]
        arena += [env[:, i, :, :].rearrange("p s t -> p (s t)") for i in range(RB)]

        def cut(i, rows=128):
            return arena[i][0:rows, :].rearrange("p (a t) -> p a t", t=SEQ)

        xi = cut(0)[:, 0:2]
        zs = cut(0)[:, 2:4]
        dt = cut(1)[:, 0:2]
        dtx = cut(1)[:, 2:4]
        Bt = cut(2)[:, 0:2]
        Ct = cut(2)[:, 2:4]
        decay = cut(3)
        drive = cut(4)
        state = cut(5)
        hc = cut(6)
        gated = cut(7)[:, 0:1]
        sp = cut(7)[:, 1:4]
        sp2 = cut(8)[:, 0:2]
        cvt = cut(8, D)[:, 2:4]
        ln_a = cut(9, D)
        ln_b = cut(10, D)
        hacc = cut(11, D)
        wrow = pos_sb[:, 0:1, :]
        bits = [hot_all[:, t // 2, (t % 2) * (SEQ // 2):(t % 2 + 1) * (SEQ // 2)].bitcast(BF16) for t in range(ST)]
        tie = sb("tie", [128, ST, 128], BF16)
        ones_bf = sb("ones_bf", [128, D], BF16)
        wcol = sb("wcol", [128, ST])
        ffh = pos_sb[:, 1:3, :]
        ffin = hid1[0:D, :, 0:SEQ]
        mask = hid2[:, 0, 0:SEQ]
        neg_A = sb("neg_A", [128, 2, P_DIM])
        dt_b = sb("dt_b", [128, 2])

        block = ctx.enter_context(nc.Block())

        @block.sync
        def _(sp_):
            sp_.dma_start(w64_sb[:, :], w64).then_inc(s_load[1], 16)
            sp_.dma_start(ids_sb[:, :, :], ids).then_inc(s_load[0], 16)
            sp_.dma_start(w128_sb[:, :], w128).then_inc(s_load[2], 16)
            sp_.dma_start(const_sb[:, :], const).then_inc(s_load[3], 16)
            sp_.dma_start(pos_sb[:, :, :], pos).then_inc(s_load[4], 16)
            for b in range(BATCH):
                sp_.wait_ge(S["out"], b + 1)
                sp_.dma_start(out[:, b, :], ffin[:, b % 2, :]).then_inc(s_outdma[b % 2], 16)
            for i in range(2):
                sp_.wait_ge(s_outdma[i], 16 * BATCH // 2)

        @block.tensor
        def _(pe):
            mm = nc.tensor.matmul
            for i in (1, 3):
                pe.wait_ge(s_load[i], 16)
            for j in range(TILES):
                b, t = divmod(j, ST)
                pe.wait_ge(s_hot, b + 1)
                mm(gathered[j // 6][:, (j % 6) * (D + 4):(j % 6 + 1) * (D + 4)],
                   hot[:, b, K1 // 2 + t * 128:K1 // 2 + (t + 1) * 128], w64c("embloc"),
                   start=True, stop=True).then_inc(s_gather, 1)
            pe.wait_ge(s_pad, 1)
            pe.wait_ge(s_load[2], 16)

            def conv1(b):
                if b >= 2:
                    pe.wait_ge(s_hid1, b - 1)
                for k in range(K1):
                    last = mm(conv1_ps[b % 2][:, :], tok_w1[:, k, :], hot[:, b, k:k + SEQ], start=k == 0, stop=k == K1 - 1)
                last.then_inc(s_conv1, 1)

            def conv2(b):
                pe.wait_ge(s_hid1, b + 1)
                if b >= 2:
                    pe.wait_ge(s_hid2, b - 1)
                for k in range(K2):
                    last = mm(conv2_ps[b % 2][0:D, :], tok_w2[:, k, :], hid1[:, b % 2, k:k + SEQ], start=k == 0, stop=k == K2 - 1)
                last.then_inc(s_conv2, 1)

            def conv3(b):
                pe.wait_ge(s_hid2, b + 1)
                for t in range(ST):
                    for k in range(K3):
                        last = mm(ctx_logit[:, b * ST + t:b * ST + t + 1],
                                  hid2[:, b % 2, t * 128 + k:t * 128 + k + 128], w64c("w3", k),
                                  start=k == 0, stop=k == K3 - 1)
                last.then_inc(s_conv3, 1)

            conv1(0)
            conv1(1)
            for b in range(BATCH):
                conv2(b)
                if b + 2 < BATCH:
                    conv1(b + 2)
                conv3(b)

            for j in range(TILES):
                b, t = divmod(j, ST)
                if t == 0:
                    pe.wait_ge(s_amps, b + 1)
                    if b >= 2:
                        pe.wait_ge(s_h1, b - 1)
                pe.wait_ge(s_wave, j + 1)
                for s in range(SCALES):
                    last = mm(field_ps[b % 2][0:D, :], amps[:, j, s, :], env[:, j % RB, s, :],
                              start=t == 0 and s == 0, stop=t == ST - 1 and s == SCALES - 1)
                last.then_inc(s_field, 1)
            pe.wait_ge(s_h1, BATCH)

            def fill(product, v, rows, pairs):
                k = FILL[product, v]
                if k >= 2:
                    pe.wait_ge(s_evac[k % 2], k // 2)
                for i, (lhsT, rhs) in enumerate(pairs):
                    last = mm(shared[k % 2][0:rows, 0:rhs.shape[-1]], lhsT, rhs, start=i == 0, stop=i == len(pairs) - 1)
                last.then_inc(s_fill[k % 2], 1)

            def small(name, v):
                d, b = divmod(v, BATCH)
                D_ = "fb"[d]
                if name == "ln1_mean":
                    fill("m1", v, D, [(mean64, h1[:, b, :])])
                elif name == "ln1_var":
                    pe.wait_ge(S["sq1"], b + 1)
                    fill("v1", v, D, [(mean64, ln_b[:, 0, :])])
                elif name == "in_proj":
                    if d == 0:
                        pe.wait_ge(S["xn"], b + 1)
                        x = xn[:, b, 1:SEQ + 1]
                    else:
                        pe.wait_ge(S["y1n"], b + 1)
                        x = y1n[:, b, :]
                    fill("xi", v, 128, [(w64c(D_ + "_in_wx"), x)])
                    fill("z", v, 128, [(w64c(D_ + "_in_wz"), x)])
                elif name == "x_proj":
                    evacuated(pe, "xi", v)
                    fill("dt", v, 128, [(w128c(D_ + "_xp_dt"), xi[:, v % 2, :])])
                    fill("B", v, 128, [(w128c(D_ + "_xp_B"), xi[:, v % 2, :])])
                elif name == "x_proj_C":
                    fill("C", v, 128, [(w128c(D_ + "_xp_C"), xi[:, v % 2, :])])
                elif name == "out_proj":
                    pe.wait_ge(S["gate"], v + 1)
                    fill("o", v, D, [(w128c(D_ + "_out_w"), gated[:, 0, :])])
                elif name == "ln2_mean":
                    evacuated(pe, "o", v)
                    fill("m2", v, D, [(mean64, ln_a[:, 1, :])])
                elif name == "ln2_var":
                    pe.wait_ge(S["sq2"], b + 1)
                    fill("v2", v, D, [(mean64, ln_b[:, 1, :])])
                elif name == "ln3_mean":
                    evacuated(pe, "o", v)
                    fill("m3", v, D, [(mean64, h1[:, b, :])])
                elif name == "ln3_var":
                    pe.wait_ge(S["sq3"], b + 1)
                    fill("v3", v, D, [(mean64, ln_b[:, 1, :])])
                elif name == "ffn_route":
                    pe.wait_ge(S["xn3"], b + 1)
                    fill("w", v, 128, [(w64c("wr"), xn[:, b, 1:SEQ + 1])])
                elif name == "ffn_col":
                    evacuated(pe, "w", v)
                    k = FILL["wc", v]
                    pe.wait_ge(s_evac[k % 2], k // 2)
                    for t in range(ST):
                        last = nc.tensor.transpose(shared[k % 2][:, t:t + 1], wrow[0:1, 0, t * 128:(t + 1) * 128], constc("one")[0:1, :])
                    last.then_inc(s_fill[k % 2], 1)
                elif name == "ffn_rank_sum":
                    pe.wait_ge(S["rankbits"], b + 1)
                    k = FILL["rank", v]
                    pe.wait_ge(s_evac[k % 2], k // 2)
                    for t in range(ST):
                        mm(shared[k % 2][0:D, :], ones_bf[:, :], bits[t], start=t == 0, stop=False, skip_group_check=True)
                        last = mm(shared[k % 2][0:D, t * 128:(t + 1) * 128], ones_bf[:, :], tie[:, t, :], start=False,
                                  stop=t == ST - 1, skip_group_check=True)
                    last.then_inc(s_fill[k % 2], 1)
                elif name == "ffn_up":
                    for i in range(2):
                        fill(f"up{i}", v, 128, [(w64c("ffn_w1")[:, i * 128:(i + 1) * 128], xn[:, b, 1:SEQ + 1])])
                elif name == "ffn_down":
                    evacuated(pe, "up0", v)
                    evacuated(pe, "up1", v)
                    w2 = w128c("ffn_w2")
                    fill("y", v, D, [(w2[:, i * D:(i + 1) * D], ffh[:, i, :]) for i in range(2)])

            def replicate(c):
                v, p = divmod(c, P_DIM)
                g, l = divmod(p, PL)
                rows = slice(32 * g, 32 * g + 32)
                if p == 0:
                    pe.wait_ge(S["dt"], v + 1)
                if c >= 2:
                    pe.wait_ge(s_decay, c - 1)
                mm(dt_rep[c % 2][:, :], sel[rows, l, :], dt[rows, v % 2, :], start=True, stop=True,
                   tile_position=(32 * g, 0)).then_inc(s_dtrep, 1)
                if p == 0:
                    pe.wait_ge(S["dtx"], v + 1)
                if c >= 2:
                    pe.wait_ge(s_drive, c - 1)
                mm(dx_rep[c % 2][:, :], sel[rows, l, :], dtx[rows, v % 2, :], start=True, stop=True,
                   tile_position=(32 * g, 0)).then_inc(s_dxrep, 1)

            def sum_n(c):
                v, p = divmod(c, P_DIM)
                g, l = divmod(p, PL)
                if p == 0 and v >= 2:
                    pe.wait_ge(S["gate"], v - 1)
                pe.wait_ge(s_hc, c + 1)
                mm(y_ps[v % 2][32 * g:32 * g + 32, :], ssum[:, l, :], hc[:, c % RC, :], start=l == 0, stop=l == PL - 1,
                   tile_position=(0, 32 * g)).then_inc(s_ysum, 1)

            for u, s in SLOTS:
                for name, v in PLAN.get((u, s), []):
                    small(name, v)
                if 0 <= u < UNITS:
                    c = u * P_DIM + s
                    replicate(c)
                    if c >= LAG:
                        sum_n(c - LAG)
                    if c == UNITS * P_DIM - 1:
                        for k in range(c - LAG + 1, c + 1):
                            sum_n(k)

        @block.vector
        def _(ve):
            v_ = nc.vector
            chain = [0]

            def link(ins):
                chain[0] += 1
                ins.then_inc(s_dve, 1)
                ve.wait_ge(s_dve, chain[0])

            v_.memset(hot[:, :, 0:K1 // 2], 0.0)
            v_.memset(hot[:, :, SEQ + K1 // 2:SEQ + K1 - 1], 0.0)
            v_.memset(hid1[:, :, 0:2], 0.0)
            v_.memset(hid1[:, :, SEQ + 2:SEQ + 4], 0.0)
            v_.memset(hid2[:, :, 0:1], 0.0)
            v_.memset(hid2[:, :, SEQ + 1:SEQ + 2], 0.0)
            v_.memset(xn[:, :, 0:1], 0.0)
            v_.memset(ones_bf[:, :], 1.0)
            v_.memset(xn[:, :, SEQ + 1:SEQ + 2], 0.0).then_inc(s_pad, 1)
            ve.wait_ge(s_load[0], 16)
            ve.wait_ge(s_load[3], 16)
            for b in range(BATCH):
                v_.tensor_scalar(hot[:, b, K1 // 2:K1 // 2 + SEQ], ids_sb[:, b, :], constc("vocab")[0:VOCAB, :], None,
                                 ALU.is_equal).then_inc(s_hot, 1)
            for k in range(3):
                n = min(6, TILES - 6 * k)
                ve.wait_ge(s_gather, 6 * k + n)
                last = v_.tensor_copy(loc[:, 6 * k:6 * k + n, :], gathered[k][:, 0:n * (D + 4)].rearrange("p (j e) -> p j e", j=n))
            chain[0] += 1
            last.then_inc(s_dve, 1)
            ve.wait_ge(s_dve, chain[0])
            ve.wait_ge(s_load[2], 16)

            def over_scales(a):
                return a.unsqueeze(2).to_broadcast([128, TILES, SCALES])

            def over_tiles(a):
                return a.unsqueeze(1).to_broadcast([128, TILES, SCALES])

            lshift, lwidth, lamp, lphase = (loc[:, :, D + k] for k in range(4))
            v_.scalar_tensor_tensor(center[:, :], lshift, 0.05, constc("place"), ALU.mult, ALU.add)
            v_.tensor_scalar(phase[:, :], lphase, 0.5, 0.25, ALU.mult, ALU.add)
            link(v_.scalar_tensor_tensor(absw[:, :], lwidth, -1.0, lwidth, ALU.mult, ALU.max))
            link(v_.tensor_tensor(width[:, :, :], over_scales(absw[:, :]), over_tiles(w128c("widths")), ALU.mult))
            link(v_.tensor_scalar(width[:, :, :], width[:, :, :], 1e-5, None, ALU.add))
            link(v_.reciprocal(inv_w[:, :, :], width[:, :, :]))
            v_.scalar_tensor_tensor(neg_half[:, :, :], inv_w[:, :, :], -0.5, inv_w[:, :, :], ALU.mult, ALU.mult).then_inc(s_param, 1)
            v_.tensor_scalar(neg_b3[:, :], w128c("b3"), -1.0, None, ALU.mult).then_inc(s_negb3, 1)
            for d in range(2):
                last = v_.tensor_tensor(dt_b[:, d:d + 1], w128c("fb"[d] + "_xp_bdt"), w128c("fb"[d] + "_dt_bias"), ALU.add)
            last.then_inc(S["bias"], 1)
            link(v_.tensor_tensor(sw2[:, :], w128c("sw"), w128c("sw"), ALU.mult))
            ve.wait_ge(s_ampexp, 1)
            link(v_.tensor_scalar(amp_den[:, :], amp_exp[:, :], 1.0, None, ALU.add))
            link(v_.reciprocal(amp_scale[:, :], amp_den[:, :]))
            link(v_.tensor_tensor(scale_w[:, :, :], over_scales(amp_scale[:, :]), over_tiles(sw2[:, :]), ALU.mult))

            ve.wait_ge(s_load[4], 16)

            def amplitudes():
                ve.wait_ge(s_ctxexp, 1)
                link(v_.tensor_scalar(ctx_den[:, :], ctx_exp[:, :], 1.0, None, ALU.add))
                link(v_.reciprocal(ctx_sig[:, :], ctx_den[:, :]))
                link(v_.tensor_tensor(ctx_w[:, :, :], over_scales(ctx_sig[:, :]), scale_w[:, :, :], ALU.mult))
                for b in range(BATCH):
                    js = slice(b * ST, (b + 1) * ST)
                    v_.tensor_tensor(amps[:, js, :, :], loc[:, js, 0:D].unsqueeze(2).to_broadcast([128, ST, SCALES, D]),
                                     ctx_w[:, js, :].unsqueeze(3).to_broadcast([128, ST, SCALES, D]), ALU.mult).then_inc(s_amps, 1)

            for j in range(TILES):
                b = j // ST
                if j >= RX:
                    ve.wait_ge(s_xd2, j - RX + 1)
                if j >= RB:
                    ve.wait_ge(s_wave, j - RB + 1)
                v_.tensor_scalar(xd[:, j % RX, :], pos_sb[:, b, :], center[:, j:j + 1], None, ALU.subtract).then_inc(s_xd, 1)
                ve.wait_ge(s_xd, j + 1)
                for s in range(SCALES):
                    last = v_.tensor_scalar(turn[:, j % RB, s, :], xd[:, j % RX, :], inv_w[:, j, s:s + 1], phase[:, j:j + 1],
                                            ALU.mult, ALU.add)
                link(last)
                link(v_.tensor_scalar(nearest[:, :, :], turn[:, j % RB, :, :], ROUND, -ROUND, ALU.add, ALU.add))
                v_.tensor_tensor(turn[:, j % RB, :, :], turn[:, j % RB, :, :], nearest[:, :, :], ALU.subtract).then_inc(s_turn, 1)
                ve.wait_ge(s_turn, j + 1)
                if j == RX - 1:
                    amplitudes()

            ve.wait_ge(s_field, TILES)
            ve.wait_ge(s_sin, TILES)
            v_.memset(decay[:, :, 0:1], 0.0).then_inc(S["A"], 1)

            def read(product, v):
                k = FILL[product, v]
                filled(ve, product, v)
                return shared[k % 2], s_evac[k % 2]

            def small(name, v):
                d, b = divmod(v, BATCH)
                D_ = "fb"[d]
                if name == "ln1_center":
                    ps, ev = read("m1", v)
                    if b:
                        ve.wait_ge(S["xn"], b)
                    v_.tensor_tensor(ln_a[:, 0, :], h1[:, b, :], ps[0:D, :], ALU.subtract).then_inc(ev, 1)
                elif name == "gate":
                    if v:
                        filled(ve, "o", v - 1)
                    ve.wait_ge(s_ysum, P_DIM * (v + 1))
                    link(v_.scalar_tensor_tensor(gated[:, 0, :], xi[:, v % 2, :], w128c(D_ + "_D_skip"), y_ps[v % 2][:, :],
                                                 ALU.mult, ALU.add))
                    v_.tensor_tensor(gated[:, 0, :], gated[:, 0, :], zs[:, v % 2, :], ALU.mult).then_inc(S["gate"], 1)
                elif name == "ln2_center":
                    ps, ev = read("m2", v)
                    v_.tensor_tensor(ln_a[:, 1, :], ln_a[:, 1, :], ps[0:D, :], ALU.subtract).then_inc(ev, 1)
                elif name == "ln2_scale":
                    ve.wait_ge(S["rstd2"], b + 1)
                    v_.scalar_tensor_tensor(ln_b[:, 1, :], ln_a[:, 1, :], w64c("norm_w"), ln_b[:, 3, :], ALU.mult, ALU.mult)\
                        .then_inc(S["sc2"], 1)
                elif name == "h2":
                    ps, ev = read("o", v)
                    ve.wait_ge(S["cgelu"], b + 1)
                    link(v_.tensor_tensor(ln_a[:, 3, :], h1[:, b, :], hacc[:, b, :], ALU.add))
                    v_.scalar_tensor_tensor(h1[:, b, :], ps[0:D, ::-1], w64c("b_out_b"), ln_a[:, 3, :], ALU.add, ALU.add)\
                        .then_inc(ev, 1)
                elif name == "ln3_center":
                    ps, ev = read("m3", v)
                    v_.tensor_tensor(ln_a[:, 2, :], h1[:, b, :], ps[0:D, :], ALU.subtract).then_inc(ev, 1)
                elif name == "ln3_out":
                    ve.wait_ge(S["rstd3"], b + 1)
                    link(v_.tensor_tensor(xn[:, b, 1:SEQ + 1], ln_a[:, 2, :], ln_b[:, 3, :], ALU.mult))
                    v_.tensor_tensor(h1[:, b, :], h1[:, b, :], xn[:, b, 1:SEQ + 1], ALU.add).then_inc(S["xn3"], 1)
                elif name == "ffn_route_copy":
                    ps, ev = read("w", v)
                    v_.tensor_scalar(wrow[:, 0, :], ps[:, :], w128c("br"), None, ALU.add).then_inc(ev, 1)
                elif name == "ffn_col_copy":
                    ps, ev = read("wc", v)
                    v_.tensor_copy(wcol[:, :], ps[:, 0:ST]).then_inc(ev, 1)
                elif name == "ffn_mask":
                    ps, ev = read("rank", v)
                    v_.scalar_tensor_tensor(mask[:, :], ps[0:D, :], CAP - 0.5, wrow[0:D, 0, :], ALU.is_lt, ALU.mult).then_inc(ev, 1)
                elif name == "ffn_rank":
                    evacuated(ve, "w", v)
                    evacuated(ve, "wc", v)
                    for t in range(ST):
                        here = slice(t * 128, (t + 1) * 128)
                        v_.tensor_scalar(bits[t][:, 0:(t + 1) * 128], wrow[:, 0, 0:(t + 1) * 128], wcol[:, t:t + 1], None, ALU.is_lt)
                        if t + 1 < ST:
                            v_.tensor_scalar(bits[t][:, (t + 1) * 128:], wrow[:, 0, (t + 1) * 128:], wcol[:, t:t + 1], None, ALU.is_le)
                        last = v_.scalar_tensor_tensor(tie[:, t, :], wrow[:, 0, here], wcol[:, t:t + 1], constc("tri"),
                                                       ALU.is_equal, ALU.mult)
                    last.then_inc(S["rankbits"], 1)
                elif name == "ffn_out":
                    ps, ev = read("y", v)
                    if b >= 2:
                        ve.wait_ge(s_outdma[b % 2], 16 * (b // 2))
                    evacuated(ve, "rank", v)
                    v_.scalar_tensor_tensor(ffin[:, b % 2, :], ps[0:D, :], w64c("ffn_b2"), mask[:, :], ALU.add, ALU.mult)\
                        .then_inc(ev, 1)
                    evacuated(ve, "y", v)
                    v_.tensor_tensor(ffin[:, b % 2, :], ffin[:, b % 2, :], h1[:, b, :], ALU.add).then_inc(S["out"], 1)

            def drive_step(c):
                v = c // P_DIM
                if c % P_DIM == 0:
                    evacuated(ve, "B", v)
                ve.wait_ge(s_dxrep, c + 1)
                v_.tensor_tensor(drive[:, c % RC, :], dx_rep[c % 2][:, :], Bt[:, v % 2, :], ALU.mult).then_inc(s_drive, 1)

            def scan_step(c):
                ve.wait_ge(s_decay, c + 1)
                ve.wait_ge(s_drive, c + 1)
                if c >= RC:
                    ve.wait_ge(s_hc, c - RC + 1)
                v_.tensor_tensor_scan(state[:, c % RC, :], decay[:, c % RC, :], drive[:, c % RC, :], 0.0,
                                      ALU.mult, ALU.add).then_inc(s_state, 1)

            for u, s in SLOTS:
                for name, v in PLAN.get((u, s), []):
                    small(name, v)
                if 0 <= u < UNITS:
                    c = u * P_DIM + s
                    drive_step(c)
                    if c >= 1:
                        scan_step(c - 1)
                    if c == UNITS * P_DIM - 1:
                        scan_step(c)

        @block.scalar
        def _(ac):
            act = nc.scalar.activation
            chain = [0]

            def link(ins):
                chain[0] += 1
                ins.then_inc(s_act, 1)
                ac.wait_ge(s_act, chain[0])

            ac.wait_ge(s_load[2], 16)
            ac.wait_ge(s_load[3], 16)
            for d in range(2):
                last = act(neg_A[:, d, :], w128c("fb"[d] + "_A_log"), ACT.Exp)
            link(last)
            link(act(neg_A[:, :, :], neg_A[:, :, :], ACT.Copy, scale=-1.0))
            ac.wait_ge(s_param, 1)
            act(amp_exp[:, :], loc[:, :, D + 2], ACT.Exp, scale=-1.0).then_inc(s_ampexp, 1)
            ac.wait_ge(s_negb3, 1)

            def hidden1(b):
                ac.wait_ge(s_conv1, b + 1)
                if b >= 2:
                    ac.wait_ge(s_conv2, b - 1)
                act(hid1[:, b % 2, 2:2 + SEQ], conv1_ps[b % 2][:, :], ACT.Gelu, bias=w128c("tok_b1")).then_inc(s_hid1, 1)

            def hidden2(b):
                ac.wait_ge(s_conv2, b + 1)
                if b >= 2:
                    ac.wait_ge(s_conv3, b - 1)
                act(hid2[:, b % 2, 1:1 + SEQ], conv2_ps[b % 2][0:D, :], ACT.Gelu, bias=w64c("b2")).then_inc(s_hid2, 1)

            def envelopes(b):
                for j in range(b * ST, (b + 1) * ST):
                    ac.wait_ge(s_xd, j + 1)
                    if j >= 2:
                        ac.wait_ge(s_env, j - 1)
                    act(xd2[:, j % 2, :], xd[:, j % RX, :], ACT.Square).then_inc(s_xd2, 1)
                    ac.wait_ge(s_xd2, j + 1)
                    if j >= RB:
                        ac.wait_ge(s_field, j - RB + 1)
                    for s in range(SCALES):
                        last = act(env[:, j % RB, s, :], xd2[:, j % 2, :], ACT.Exp, scale=neg_half[:, j, s:s + 1])
                    last.then_inc(s_env, 1)

            def waves(b):
                for j in range(b * ST, (b + 1) * ST):
                    ac.wait_ge(s_turn, j + 1)
                    act(turn[:, j % RB, :, :], turn[:, j % RB, :, :], ACT.Sin, scale=TWO_PI).then_inc(s_sin, 1)

            def field_out(b):
                ac.wait_ge(s_field, ST * (b + 1))
                act(h1[:, b, :], field_ps[b % 2][0:D, :], ACT.Copy).then_inc(s_h1, 1)

            envelopes(0)
            hidden1(0)
            hidden1(1)
            for b in range(BATCH):
                hidden2(b)
                if b + 2 < BATCH:
                    hidden1(b + 2)
            ac.wait_ge(s_conv3, BATCH)
            act(ctx_exp[:, :], ctx_logit[:, 0:TILES], ACT.Exp, bias=neg_b3[:, :], scale=-1.0).then_inc(s_ctxexp, 1)
            waves(0)
            waves(1)
            envelopes(1)
            envelopes(2)
            field_out(0)
            waves(2)
            waves(3)
            field_out(1)
            envelopes(3)
            field_out(2)
            field_out(3)
            ac.wait_ge(S["A"], 1)
            ac.wait_ge(S["bias"], 1)

            def read(product, v):
                k = FILL[product, v]
                filled(ac, product, v)
                return shared[k % 2], s_evac[k % 2]

            def rstd(product, v, out_):
                ps, ev = read(product, v)
                act(out_, ps[0:D, :], ACT.Ln, bias=constc("eps")[0:D, :]).then_inc(ev, 1)
                evacuated(ac, product, v)

            def small(name, v):
                d, b = divmod(v, BATCH)
                D_ = "fb"[d]
                if name == "ln1_square":
                    evacuated(ac, "m1", v)
                    act(ln_b[:, 0, :], ln_a[:, 0, :], ACT.Square).then_inc(S["sq1"], 1)
                elif name == "ln1_rstd":
                    rstd("v1", v, ln_b[:, 2, :])
                    act(ln_b[:, 2, :], ln_b[:, 2, :], ACT.Exp, scale=-0.5).then_inc(S["rstd1"], 1)
                elif name == "silu":
                    if v >= 2:
                        ac.wait_ge(S["gate"], v - 1)
                    for product, bias, to in (("xi", "_in_bx", xi), ("z", "_in_bz", zs)):
                        ps, ev = read(product, v)
                        act(to[:, v % 2, :], ps[:, :], ACT.Silu, bias=w128c(D_ + bias)).then_inc(ev, 1)
                elif name == "softplus":
                    ps, ev = read("dt", v)
                    if v:
                        ac.wait_ge(S["dt"], v)
                    link(act(sp[:, 0, :], ps[:, :], ACT.Abs, bias=dt_b[:, d:d + 1]))
                    act(sp[:, 1, :], ps[:, :], ACT.Relu, bias=dt_b[:, d:d + 1]).then_inc(ev, 1)
                    link(act(sp[:, 0, :], sp[:, 0, :], ACT.Exp, scale=-1.0))
                    act(sp[:, 2, :], sp[:, 0, :], ACT.Ln, bias=constc("one")).then_inc(S["sp_parts"], 1)
                    ps, ev = read("B", v)
                    if v >= 2:
                        ac.wait_ge(s_drive, P_DIM * (v - 1))
                    act(Bt[:, v % 2, :], ps[:, :], ACT.Identity, bias=w128c(D_ + "_xp_bB")).then_inc(ev, 1)
                elif name == "dt":
                    ps, ev = read("C", v)
                    if v >= 2:
                        ac.wait_ge(s_hc, P_DIM * (v - 1))
                    act(Ct[:, v % 2, :], ps[:, :], ACT.Identity, bias=w128c(D_ + "_xp_bC")).then_inc(ev, 1)
                elif name == "out_bias":
                    ps, ev = read("o", v)
                    if b:
                        ac.wait_ge(S["sc2"], b)
                    act(ln_a[:, 1, :], ps[0:D, :], ACT.Identity, bias=w64c("f_out_b")).then_inc(ev, 1)
                elif name == "ln2_square":
                    evacuated(ac, "m2", v)
                    act(ln_b[:, 1, :], ln_a[:, 1, :], ACT.Square).then_inc(S["sq2"], 1)
                elif name == "ln2_rstd":
                    rstd("v2", v, ln_b[:, 3, :])
                    act(ln_b[:, 3, :], ln_b[:, 3, :], ACT.Exp, scale=-0.5).then_inc(S["rstd2"], 1)
                elif name == "ln2_out":
                    ac.wait_ge(S["sc2"], b + 1)
                    act(y1n[:, b, ::-1], ln_b[:, 1, :], ACT.Identity, bias=w64c("norm_b")).then_inc(S["y1n"], 1)
                elif name == "ln3_square":
                    evacuated(ac, "m3", v)
                    act(ln_b[:, 1, :], ln_a[:, 2, :], ACT.Square).then_inc(S["sq3"], 1)
                elif name == "ln3_rstd":
                    if b:
                        ac.wait_ge(S["xn3"], b)
                    rstd("v3", v, ln_b[:, 3, :])
                    act(ln_b[:, 3, :], ln_b[:, 3, :], ACT.Exp, scale=-0.5).then_inc(S["rstd3"], 1)
                elif name == "conv_gelu":
                    ac.wait_ge(S["conv"], b + 1)
                    act(hacc[:, b, :], hacc[:, b, :], ACT.Gelu, bias=w64c("conv_b")).then_inc(S["cgelu"], 1)
                elif name == "ffn_gelu":
                    if b:
                        filled(ac, "y", v - 1)
                    for i in range(2):
                        ps, ev = read(f"up{i}", v)
                        act(ffh[:, i, :], ps[:, :], ACT.Gelu_apprx_tanh, bias=w128c("ffn_b1", i)).then_inc(ev, 1)

            def decay_step(c):
                d, p = c // P_DIM // BATCH, c % P_DIM
                ac.wait_ge(s_dtrep, c + 1)
                if c >= RC:
                    ac.wait_ge(s_state, c - RC + 1)
                act(decay[:, c % RC, 1:], dt_rep[c % 2][:, 1:], ACT.Exp, scale=neg_A[:, d, p:p + 1]).then_inc(s_decay, 1)

            for u, s in SLOTS:
                for name, v in PLAN.get((u, s), []):
                    small(name, v)
                if 0 <= u < UNITS:
                    decay_step(u * P_DIM + s)

        @block.gpsimd
        def _(po):
            tt, stt, ts = nc.gpsimd.tensor_tensor, nc.gpsimd.scalar_tensor_tensor, nc.gpsimd.tensor_scalar
            chain = [0]

            def link(ins):
                chain[0] += 1
                ins.then_inc(s_pool, 1)
                po.wait_ge(s_pool, chain[0])

            for j in range(TILES):
                po.wait_ge(s_env, j + 1)
                po.wait_ge(s_sin, j + 1)
                tt(env[:, j % RB, :, :], env[:, j % RB, :, :], turn[:, j % RB, :, :], ALU.mult).then_inc(s_wave, 1)

            def small(name, v):
                d, b = divmod(v, BATCH)
                if name == "ln1_out":
                    po.wait_ge(S["rstd1"], b + 1)
                    tt(xn[:, b, 1:SEQ + 1], ln_a[:, 0, :], ln_b[:, 2, :], ALU.mult).then_inc(S["xn"], 1)
                elif name == "dt":
                    po.wait_ge(S["sp_parts"], v + 1)
                    link(ts(sp2[:, 0, :], sp[:, 0, :], 1.0, -1.0, ALU.add, ALU.add))
                    link(tt(sp2[:, 0, :], sp[:, 0, :], sp2[:, 0, :], ALU.subtract))
                    link(tt(sp2[:, 0, :], sp2[:, 0, :], sp[:, 2, :], ALU.add))
                    if v >= 2:
                        po.wait_ge(s_dxrep, P_DIM * (v - 1))
                    tt(dt[:, v % 2, :], sp2[:, 0, :], sp[:, 1, :], ALU.add).then_inc(S["dt"], 1)
                    po.wait_ge(S["dt"], v + 1)
                    tt(dtx[:, v % 2, :], dt[:, v % 2, :], xi[:, v % 2, :], ALU.mult).then_inc(S["dtx"], 1)
                elif name == "conv":
                    link(ts(cvt[:, 0, :], xn[:, b, 0:SEQ], w64c("conv_w", 0), None, ALU.mult))
                    link(ts(cvt[:, 1, :], xn[:, b, 1:SEQ + 1], w64c("conv_w", 1), None, ALU.mult))
                    link(tt(cvt[:, 0, :], cvt[:, 0, :], cvt[:, 1, :], ALU.add))
                    link(ts(cvt[:, 1, :], xn[:, b, 2:SEQ + 2], w64c("conv_w", 2), None, ALU.mult))
                    tt(hacc[:, b, :], cvt[:, 0, :], cvt[:, 1, :], ALU.add).then_inc(S["conv"], 1)

            def read_out(c):
                v = c // P_DIM
                if c % P_DIM == 0:
                    evacuated(po, "C", v)
                po.wait_ge(s_state, c + 1)
                if c >= RC:
                    po.wait_ge(s_ysum, c - RC + 1)
                tt(hc[:, c % RC, :], state[:, c % RC, :], Ct[:, v % 2, :], ALU.mult).then_inc(s_hc, 1)

            for u, s in SLOTS:
                for name, v in PLAN.get((u, s), []):
                    small(name, v)
                if 0 <= u < UNITS:
                    read_out(u * P_DIM + s)


def constants():
    c = {}
    r = np.arange(128)
    h_r, l_r = r % 32 // PL, r % PL
    c["sel"] = ((l_r[:, None, None] == np.arange(PL)[None, :, None])
                & (h_r[:, None, None] == (r // N_DIM)[None, None, :])).reshape(128, -1)
    q = np.arange(32)
    c["ssum"] = (((r // N_DIM)[:, None, None] == (q // PL)[None, None, :])
                 & (np.arange(PL)[None, :, None] == (q % PL)[None, None, :])).reshape(128, -1)
    c["tri"] = r[:, None] < r[None, :]
    line = (np.arange(SEQ, dtype=np.float32) / np.float32(SEQ - 1)).astype(np.float32)
    c["place"] = np.tile(line.reshape(ST, 128).T, (1, BATCH))
    c["eps"] = np.full((128, 1), LN_EPS)
    c["one"] = np.ones((128, 1))
    c["mean"] = np.full((128, D), 1.0 / D)
    c["vocab"] = r[:, None]
    out = np.zeros((128, C128_N), np.float32)
    for name, (a, b) in C128.items():
        out[:, a:b] = c[name]
    return out


def kernel(**inputs):
    import concourse.bacc as bacc
    from concourse.bass_utils import run_bass_kernel_spmd

    x = {k: np.asarray(v) for k, v in inputs.items()}
    perm = np.arange(DI).reshape(HEADS, G, PL).transpose(1, 0, 2).reshape(-1)

    def row(a, p=128):
        return np.broadcast_to(a.reshape(1, -1), (p, a.size))

    p128 = {
        "tok_w2": x["L0_tok_w2"].transpose(1, 2, 0).reshape(HID, -1), "tok_b1": x["L0_tok_b1"][:, None],
        "b3": row(x["L0_tok_b3"]), "widths": row(x["L0_tok_multiscale_widths"]), "sw": row(x["L0_tok_scale_weights"]),
        "br": row(x["L0_ffn_br"]),
        "ffn_w2": x["L0_ffn_w2"].reshape(2, 128, D).transpose(1, 0, 2).reshape(128, -1),
        "ffn_b1": x["L0_ffn_b1"].reshape(2, 128).T,
    }
    p64 = {
        "embloc": np.concatenate([x["L0_tok_emb"], x["L0_tok_locality_shapes"]], 1),
        "tok_w1": x["L0_tok_w1"].transpose(1, 2, 0).reshape(VOCAB, -1), "w3": x["L0_tok_w3"][0], "b2": x["L0_tok_b2"][:, None],
        "norm_w": x["L0_attn_norm_w"][:, None], "norm_b": x["L0_attn_norm_b"][:, None],
        "conv_w": x["L0_attn_conv_w"][:, 0, :], "conv_b": x["L0_attn_conv_b"][:, None],
        "ffn_w1": x["L0_ffn_w1"], "wr": np.broadcast_to(x["L0_ffn_wr"], (D, 128)), "ffn_b2": x["L0_ffn_b2"][:, None],
    }
    for d in "fb":
        g = {k[len("L0_attn_f_"):]: v for k, v in x.items() if k.startswith(f"L0_attn_{d}_")}
        xp, xb = g["x_proj_w"][:, perm], g["x_proj_b"][:, None]
        p128 |= {
            f"{d}_xp_dt": xp[:DI][perm].T, f"{d}_xp_B": xp[DI:2 * DI].T, f"{d}_xp_C": xp[2 * DI:].T,
            f"{d}_in_bx": g["in_proj_b"][:DI][perm][:, None], f"{d}_in_bz": g["in_proj_b"][DI:][perm][:, None],
            f"{d}_xp_bdt": xb[:DI][perm], f"{d}_dt_bias": g["dt_bias"][perm][:, None],
            f"{d}_xp_bB": xb[DI:2 * DI], f"{d}_xp_bC": xb[2 * DI:], f"{d}_D_skip": g["D_skip"][perm][:, None],
            f"{d}_A_log": g["A_log"].reshape(HEADS, P_DIM, N_DIM).transpose(0, 2, 1).reshape(128, P_DIM),
            f"{d}_out_w": g["out_proj_w"][:, perm].T,
        }
        p64 |= {f"{d}_in_wx": g["in_proj_w"][:DI][perm].T, f"{d}_in_wz": g["in_proj_w"][DI:][perm].T,
                f"{d}_out_b": g["out_proj_b"][:, None]}

    def side_by_side(parts, places):
        return np.ascontiguousarray(np.concatenate([parts[n] for n in places], 1))

    arrays = {
        "ids": np.ascontiguousarray(np.broadcast_to(x["x"], (VOCAB, BATCH, SEQ))),
        "w64": side_by_side(p64, W64), "w128": side_by_side(p128, W128),
        "pos": np.ascontiguousarray(np.broadcast_to(x["fside_BS_continuous_positions"], (128, BATCH, SEQ))),
        "const": constants(),
    }
    nc = bacc.Bacc("TRN2", target_bir_lowering=False, num_devices=1)
    args = [nc.dram_tensor(n, a.shape, mybir.dt.from_np(a.dtype), kind="ExternalInput").ap() for n, a in arrays.items()]
    out = nc.dram_tensor("out", (D, BATCH, SEQ), F32, kind="ExternalOutput").ap()
    build(nc, *args, out)
    r = run_bass_kernel_spmd(nc, [arrays], core_ids=[0])
    return r.results[0]["out"].transpose(1, 2, 0)
```

```python
from contextlib import ExitStack

import numpy as np

import concourse.bass as bass
from concourse import mybir

ALU = mybir.AluOpType
ACT = mybir.ActivationFunctionType
F32 = mybir.dt.float32
BF16 = mybir.dt.bfloat16
I32 = mybir.dt.int32

BATCH, SEQ, D = 4, 512, 64
VOCAB = 64
HID = 128
K1, K2, K3 = 7, 5, 3
KD = 3
SCALES = 4
ST = SEQ // 128
TILES = BATCH * ST
DI, HEADS, P_DIM, N_DIM = 128, 8, 16, 16
G = 4
PL = P_DIM // G
FF = 256
CAP = SEQ // 2 - 1
UNITS = 2 * BATCH
LN_EPS = 1e-5
ROUND = 1.5 * 2.0 ** 23
TWO_PI = 6.283185

RE = 8
RT = 4
RX = 3
SPLITS = 3
PAIRS = (K1 + 1) // 2
RC = 4
LAG = 3


def columns(parts):
    at, out = 0, {}
    for name, n in parts:
        out[name] = (at, at + n)
        at += n
    return out, at


W128, W128_N = columns(
    [("tok_w1", PAIRS * HID), ("embloc", D + 4), ("tok_w2", K2 * D), ("tok_b1", 1), ("b3", 1), ("widths", SCALES), ("sw", SCALES), ("br", 1),
     ("ffn_w2", 2 * D), ("ffn_b1", 2)]
    + [(f"{d}_{n}", k) for d in "fb" for n, k in
       (("xp_dt", DI), ("xp_B", DI), ("xp_C", DI), ("in_bx", 1), ("in_bz", 1), ("xp_bdt", 1), ("dt_bias", 1),
        ("xp_bB", 1), ("xp_bC", 1), ("D_skip", 1), ("A_log", P_DIM), ("out_w", D))])
W64, W64_N = columns(
    [("w3", K3), ("b2", 1), ("norm_w", 1), ("norm_b", 1),
     ("conv_w", KD), ("conv_b", 1), ("ffn_w1", FF), ("wr", 128), ("ffn_b2", 1)]
    + [(f"{d}_{n}", k) for d in "fb" for n, k in (("in_wx", DI), ("in_wz", DI), ("out_b", 1))])
C128, C128_N = columns(
    [("sel", PL * 128), ("ssum", PL * 32), ("tri", 128), ("place", TILES), ("eps", 1), ("one", 1), ("mean", D),
     ("eye", D), ("vocab", 1)])


def make_plan():
    plan = {}

    def add(u, slot, name, v):
        plan.setdefault((u, slot), []).append((name, v))

    def ln1(v, u, s):
        for k, n in enumerate(("ln1_mean", "ln1_center", "ln1_square", "ln1_var", "ln1_rstd", "ln1_out")):
            add(u, s + k, n, v)

    def front(v, u, s):
        for k, n in ((0, "in_proj"), (1, "silu"), (2, "x_proj"), (3, "softplus"), (4, "x_proj_C"), (4, "dt_sum"),
                     (5, "split_hi"), (6, "split_rest"), (7, "split_mid"), (8, "split_lo")):
            add(u, s + k, n, v)

    def post(v, u, s):
        names = [(0, "gate"), (1, "out_proj")]
        if v < BATCH:
            names += [(2, "out_bias"), (4, "ln2_mean"), (5, "ln2_center"), (6, "ln2_square"), (7, "ln2_var"),
                      (8, "ln2_rstd"), (9, "ln2_scale"), (10, "ln2_out")]
        else:
            names += [(2, "h2"), (4, "ln3_mean"), (5, "ln3_center"), (6, "ln3_square"), (7, "ln3_var"),
                      (8, "ln3_rstd"), (9, "ln3_out")]
        for k, n in names:
            add(u, s + k, n, v)

    def ffn(v, u, s):
        for k, n in ((0, "ffn_route"), (1, "ffn_route_copy"), (2, "ffn_col"), (3, "ffn_col_copy"), (4, "ffn_rank"),
                     (10, "ffn_rank_sum"), (11, "ffn_mask"), (12, "ffn_up"), (13, "ffn_gelu"), (14, "ffn_down"),
                     (15, "ffn_out")):
            add(u, s + k, n, v)

    ln1(0, -1, 0)
    front(0, -1, 6)
    ln1(1, -1, 10)
    for v in range(UNITS):
        if v + 1 < UNITS:
            front(v + 1, v, 4)
        if v >= 1:
            post(v - 1, v, 4)
        if v + 2 < BATCH:
            ln1(v + 2, v, 10)
        if v < BATCH:
            add(v, 0, "conv", v)
            add(v, 1, "conv_out", v)
        if v == BATCH:
            add(v, 15, "conv_gelu", v)
        if v - 2 >= BATCH:
            ffn(v - 2, v, 0)
    post(UNITS - 1, UNITS, 0)
    ffn(UNITS - 2, UNITS, 0)
    ffn(UNITS - 1, UNITS, 16)
    slots = [(-1, s) for s in range(16)] + [(u, s) for u in range(UNITS) for s in range(P_DIM)]
    slots += [(UNITS, s) for s in range(32)]
    return plan, slots


PLAN, SLOTS = make_plan()
SHARED_FILLS = {"ln1_mean": ["m1"], "ln1_var": ["v1"], "in_proj": ["xi", "z"], "x_proj": ["dt", "B"],
                "x_proj_C": ["C"], "out_proj": ["o"], "ln2_mean": ["m2"], "ln2_var": ["v2"], "ln3_mean": ["m3"],
                "ln3_var": ["v3"], "ffn_route": ["w"], "ffn_col": ["wc"], "ffn_rank_sum": ["rank"],
                "ffn_up": ["up0", "up1"], "ffn_down": ["y"], "conv": ["cv"]}


def number_fills():
    out, k = {}, 0
    for slot in SLOTS:
        for name, v in PLAN.get(slot, []):
            for product in SHARED_FILLS.get(name, []):
                out[product, v] = k
                k += 1
    return out


FILL = number_fills()


def build(nc, ids, w64, w128, pos, const, out):
    with ExitStack() as ctx:
        def sb(name, shape, dt=F32):
            return ctx.enter_context(nc.sbuf_tensor(name, shape, dt))

        def sem(name):
            return ctx.enter_context(nc.semaphore(name))

        bank = [ctx.enter_context(nc.psum_tensor(f"bank{i}", [128, 512], F32)) for i in range(8)]
        gathered, ctx_logit, conv_ps, field_ps = bank[0:3], bank[3], bank[4:8], bank[0:2]
        dt_rep, dx_rep, y_ps, shared = bank[0:2], bank[2:4], bank[4:6], bank[6:8]

        ids_sb = sb("ids_sb", [128, BATCH, SEQ], I32)
        w64_sb = sb("w64_sb", [64, W64_N])
        w128_sb = sb("w128_sb", [128, W128_N])
        const_sb = sb("const_sb", [128, C128_N])
        pos_sb = sb("pos_sb", [128, BATCH, SEQ])

        def w64c(name, k=None):
            a, b = W64[name]
            return w64_sb[:, a:b] if k is None else w64_sb[:, a + k:a + k + 1]

        def w128c(name, k=None):
            a, b = W128[name]
            return w128_sb[:, a:b] if k is None else w128_sb[:, a + k:a + k + 1]

        def constc(name):
            a, b = C128[name]
            return const_sb[:, a:b]

        tok_w2 = w128c("tok_w2").rearrange("c (k o) -> c k o", k=K2)
        sel = constc("sel").rearrange("r (l n) -> r l n", l=PL)
        ssum = constc("ssum").rearrange("r (l n) -> r l n", l=PL)
        mean64 = constc("mean")[0:D, :]

        hot = sb("hot", [128, BATCH, SEQ + K1 - 1], BF16)
        first = w128_sb[:, 0:PAIRS * HID + D + 4]
        first_rest = sb("first_rest", [128, 2, PAIRS * HID + D + 4])
        first_split = sb("first_split", [128, SPLITS, PAIRS * HID + D + 4], BF16)
        loc = sb("loc", [128, TILES, D + 4])
        center = sb("center", [128, TILES])
        absw = sb("absw", [128, TILES])
        phase = sb("phase", [128, TILES])
        width = sb("width", [128, TILES, SCALES])
        inv_w = sb("inv_w", [128, TILES, SCALES])
        neg_half = sb("neg_half", [128, TILES, SCALES])
        amp_exp = sb("amp_exp", [128, TILES])
        amp_den = sb("amp_den", [128, TILES])
        amp_scale = sb("amp_scale", [128, TILES])
        sw2 = sb("sw2", [128, SCALES])
        scale_w = sb("scale_w", [128, TILES, SCALES])
        neg_b3 = sb("neg_b3", [128, 1])
        ctx_exp = sb("ctx_exp", [128, TILES])
        ctx_den = sb("ctx_den", [128, TILES])
        ctx_sig = sb("ctx_sig", [128, TILES])
        ctx_w = sb("ctx_w", [128, TILES, SCALES])
        amps = sb("amps", [128, TILES, SCALES, D])
        hid1 = sb("hid1", [HID, BATCH, SEQ + K2 - 1])
        hid2 = amps[0:D, :, :, :].rearrange("p j s e -> p (j s e)")[:, 0:BATCH * (SEQ + K3 - 1)].rearrange(
            "p (b t) -> p b t", b=BATCH)
        xd = sb("xd", [128, RX, SEQ])
        xd2 = sb("xd2", [128, 2, SEQ])
        nearest = sb("nearest", [128, SCALES, SEQ])
        turn = sb("turn", [128, RT, SCALES, SEQ])
        env = sb("env", [128, RE, SCALES, SEQ])

        h1 = sb("h1", [D, BATCH, SEQ])
        xn = sb("xn", [D, BATCH, SEQ + 2])
        y1n = ids_sb[0:D, :, :].bitcast(F32)

        s_load = [sem(f"s_load{i}") for i in range(5)]
        s_hot = sem("s_hot")
        s_first = sem("s_first")
        s_firsthi = sem("s_firsthi")
        s_pad = sem("s_pad")
        s_gather = sem("s_gather")
        s_ampexp = sem("s_ampexp")
        s_param = sem("s_param")
        s_wgt = sem("s_wgt")
        s_conv1 = sem("s_conv1")
        s_hid1 = sem("s_hid1")
        s_conv2 = sem("s_conv2")
        s_hid2 = sem("s_hid2")
        s_conv3 = sem("s_conv3")
        s_negb3 = sem("s_negb3")
        s_ctxexp = sem("s_ctxexp")
        s_amps = sem("s_amps")
        s_xd = sem("s_xd")
        s_xd2 = sem("s_xd2")
        s_turn = sem("s_turn")
        s_env = sem("s_env")
        s_sin = sem("s_sin")
        s_wave = sem("s_wave")
        s_field = sem("s_field")
        s_fielddone = sem("s_fielddone")
        s_h1 = sem("s_h1")
        s_dve = sem("s_dve")
        s_act = sem("s_act")
        s_fill = [sem("s_fill0"), sem("s_fill1")]
        s_evac = [sem("s_evac0"), sem("s_evac1")]

        def filled(eng, product, v):
            eng.wait_ge(s_fill[FILL[product, v] % 2], FILL[product, v] // 2 + 1)

        def evacuated(eng, product, v):
            eng.wait_ge(s_evac[FILL[product, v] % 2], FILL[product, v] // 2 + 1)

        names = ("sq1 rstd1 xn sp_parts dt dtx hi rest mid lo gate sq2 rstd2 sc2 y1n cgelu sq3 rstd3 xn3 rankbits out bias "
                 "A sel diag").split()
        S = {n: sem("s_" + n) for n in names}
        s_stack = [sem("s_stack0"), sem("s_stack1")]
        s_outdma = [sem("s_outdma0"), sem("s_outdma1")]
        s_dtrep = sem("s_dtrep")
        s_dxrep = sem("s_dxrep")
        s_decay = sem("s_decay")
        s_drive = sem("s_drive")
        s_state = sem("s_state")
        s_hc = sem("s_hc")
        s_ysum = sem("s_ysum")

        arena = [turn[:, i, :, :].rearrange("p s t -> p (s t)") for i in range(RT)]
        arena += [env[:, i, :, :].rearrange("p s t -> p (s t)") for i in range(RE)]

        def cut(i, rows=128):
            return arena[i][0:rows, :].rearrange("p (a t) -> p a t", t=SEQ)

        xi = cut(0)[:, 0:2]
        zs = cut(0)[:, 2:4]
        dt = cut(1)[:, 0:1]
        dtx = cut(1)[:, 1:2]
        rest = cut(1)[:, 2:4]
        part = nearest[:, :, :].rearrange("p s t -> p (s t)").bitcast(BF16).rearrange("p (q j t) -> p q j t", q=2, t=SEQ)
        stack = amps[:, :, :, :].rearrange("p j s e -> p (j s e)").bitcast(BF16).rearrange(
            "p (q u g t) -> p q u g t", q=2, u=2, g=G)
        Bt = cut(2)[:, 0:2]
        Ct = cut(2)[:, 2:4]
        decay = cut(3)
        drive = cut(4)
        state = cut(5)
        hc = cut(6)
        gated = cut(7)[:, 0:1]
        sp = cut(7)[:, 1:4]
        sp2 = cut(8)[:, 0:2]
        ln_a = cut(9, D)
        ln_b = cut(10, D)
        hacc = cut(11, D)
        wrow = pos_sb[:, 0:1, :]
        bits = [hot[:, t, 0:SEQ] for t in range(ST)]
        tie = sb("tie", [128, ST, 128], BF16)
        ones_bf = sb("ones_bf", [128, D], BF16)
        wcol = sb("wcol", [128, ST])
        ffh = pos_sb[:, 1:3, :]
        ffin = hid1[0:D, :, 0:SEQ]
        mask = hid1[0:D, 2, 0:SEQ]
        sel_bf = sb("sel_bf", [SPLITS * 32, PL, 128], BF16)
        diag = sb("diag", [D, KD, D])
        neg_A = sb("neg_A", [128, 2, P_DIM])
        dt_b = sb("dt_b", [128, 2])

        block = ctx.enter_context(nc.Block())

        @block.sync
        def _(sp_):
            sp_.dma_start(w128_sb[:, :], w128).then_inc(s_load[2], 16)
            sp_.dma_start(const_sb[:, :], const).then_inc(s_load[3], 16)
            sp_.dma_start(ids_sb[:, :, :], ids).then_inc(s_load[0], 16)
            sp_.dma_start(w64_sb[:, :], w64).then_inc(s_load[1], 16)
            sp_.dma_start(pos_sb[:, :, :], pos).then_inc(s_load[4], 16)
            for v in range(UNITS):
                for j, ready in enumerate(("hi", "mid", "lo")):
                    sp_.wait_ge(S[ready], 2 * v + 2)
                    if v >= 2 and j == 0:
                        sp_.wait_ge(s_dtrep, P_DIM * (v - 1))
                        sp_.wait_ge(s_dxrep, P_DIM * (v - 1))
                    for g in range(G):
                        sp_.dma_start(stack[32 * j:32 * j + 32, :, v % 2, g, :], part[32 * g:32 * g + 32, :, j, :])\
                           .then_inc(s_stack[v % 2], 16)
            for b in range(BATCH):
                sp_.wait_ge(S["out"], b + 1)
                sp_.dma_start(out[:, b, :], ffin[:, b % 2, :]).then_inc(s_outdma[b % 2], 16)
            for i in range(2):
                sp_.wait_ge(s_outdma[i], 16 * BATCH // 2)

        @block.tensor
        def _(pe):
            mm = nc.tensor.matmul
            pe.wait_ge(s_first, 1)
            for j in range(TILES):
                b, t = divmod(j, ST)
                pe.wait_ge(s_hot, 2 * b + 2)
                for i in range(SPLITS):
                    last = mm(gathered[j // 6][:, (j % 6) * (D + 4):(j % 6 + 1) * (D + 4)],
                              hot[0:VOCAB, b, K1 // 2 + t * 128:K1 // 2 + (t + 1) * 128],
                              first_split[0:VOCAB, i, PAIRS * HID:], start=i == 0, stop=i == SPLITS - 1)
                last.then_inc(s_gather, 1)
            pe.wait_ge(s_pad, 1)

            def conv1(b):
                for k in range(PAIRS):
                    for i in range(SPLITS):
                        last = mm(conv_ps[b][:, :], first_split[:, i, k * HID:(k + 1) * HID], hot[:, b, 2 * k:2 * k + SEQ],
                                  start=k == 0 and i == 0, stop=k == PAIRS - 1 and i == SPLITS - 1)
                last.then_inc(s_conv1, 1)

            def conv2(b):
                pe.wait_ge(s_hid1, b + 1)
                for k in range(K2):
                    last = mm(conv_ps[b][0:D, :], tok_w2[:, k, :], hid1[:, b, k:k + SEQ], start=k == 0, stop=k == K2 - 1)
                last.then_inc(s_conv2, 1)

            def conv3(b):
                if b == 0:
                    pe.wait_ge(s_load[1], 16)
                pe.wait_ge(s_hid2, b + 1)
                for t in range(ST):
                    for k in range(K3):
                        last = mm(ctx_logit[:, b * ST + t:b * ST + t + 1],
                                  hid2[:, b, t * 128 + k:t * 128 + k + 128], w64c("w3", k),
                                  start=k == 0, stop=k == K3 - 1)
                last.then_inc(s_conv3, 1)

            for conv in (conv1, conv2, conv3):
                for b in range(BATCH):
                    conv(b)

            for j in range(TILES):
                b, t = divmod(j, ST)
                if t == 0:
                    pe.wait_ge(s_amps, b + 1)
                    if b >= 2:
                        pe.wait_ge(s_h1, b - 1)
                pe.wait_ge(s_wave, j + 1)
                for s in range(SCALES):
                    last = mm(field_ps[b % 2][0:D, :], amps[:, j, s, :], env[:, j % RE, s, :],
                              start=t == 0 and s == 0, stop=t == ST - 1 and s == SCALES - 1)
                last.then_inc(s_field, 1)
            pe.wait_ge(s_h1, BATCH)
            pe.wait_ge(S["sel"], 1)

            def fill(product, v, rows, pairs):
                k = FILL[product, v]
                if k >= 2:
                    pe.wait_ge(s_evac[k % 2], k // 2)
                for i, (lhsT, rhs) in enumerate(pairs):
                    last = mm(shared[k % 2][0:rows, 0:rhs.shape[-1]], lhsT, rhs, start=i == 0, stop=i == len(pairs) - 1)
                last.then_inc(s_fill[k % 2], 1)

            def small(name, v):
                d, b = divmod(v, BATCH)
                D_ = "fb"[d]
                if name == "ln1_mean":
                    fill("m1", v, D, [(mean64, h1[:, b, :])])
                elif name == "conv":
                    pe.wait_ge(S["diag"], 1)
                    fill("cv", v, D, [(diag[:, k, :], xn[:, b, k:k + SEQ]) for k in range(KD)])
                elif name == "ln1_var":
                    pe.wait_ge(S["sq1"], b + 1)
                    fill("v1", v, D, [(mean64, ln_b[:, 0, :])])
                elif name == "in_proj":
                    if d == 0:
                        pe.wait_ge(S["xn"], b + 1)
                        x = xn[:, b, 1:SEQ + 1]
                    else:
                        pe.wait_ge(S["y1n"], b + 1)
                        x = y1n[:, b, :]
                    fill("xi", v, 128, [(w64c(D_ + "_in_wx"), x)])
                    fill("z", v, 128, [(w64c(D_ + "_in_wz"), x)])
                elif name == "x_proj":
                    evacuated(pe, "xi", v)
                    fill("dt", v, 128, [(w128c(D_ + "_xp_dt"), xi[:, v % 2, :])])
                    fill("B", v, 128, [(w128c(D_ + "_xp_B"), xi[:, v % 2, :])])
                elif name == "x_proj_C":
                    fill("C", v, 128, [(w128c(D_ + "_xp_C"), xi[:, v % 2, :])])
                elif name == "out_proj":
                    pe.wait_ge(S["gate"], v + 1)
                    fill("o", v, D, [(w128c(D_ + "_out_w"), gated[:, 0, :])])
                elif name == "ln2_mean":
                    evacuated(pe, "o", v)
                    fill("m2", v, D, [(mean64, ln_a[:, 1, :])])
                elif name == "ln2_var":
                    pe.wait_ge(S["sq2"], b + 1)
                    fill("v2", v, D, [(mean64, ln_b[:, 1, :])])
                elif name == "ln3_mean":
                    evacuated(pe, "o", v)
                    fill("m3", v, D, [(mean64, h1[:, b, :])])
                elif name == "ln3_var":
                    pe.wait_ge(S["sq3"], b + 1)
                    fill("v3", v, D, [(mean64, ln_b[:, 1, :])])
                elif name == "ffn_route":
                    pe.wait_ge(S["xn3"], b + 1)
                    fill("w", v, 128, [(w64c("wr"), xn[:, b, 1:SEQ + 1])])
                elif name == "ffn_col":
                    evacuated(pe, "w", v)
                    k = FILL["wc", v]
                    pe.wait_ge(s_evac[k % 2], k // 2)
                    for t in range(ST):
                        last = nc.tensor.transpose(shared[k % 2][:, t:t + 1], wrow[0:1, 0, t * 128:(t + 1) * 128], constc("one")[0:1, :])
                    last.then_inc(s_fill[k % 2], 1)
                elif name == "ffn_rank_sum":
                    pe.wait_ge(S["rankbits"], b + 1)
                    k = FILL["rank", v]
                    pe.wait_ge(s_evac[k % 2], k // 2)
                    for t in range(ST):
                        mm(shared[k % 2][0:D, :], ones_bf[:, :], bits[t], start=t == 0, stop=False, skip_group_check=True)
                        last = mm(shared[k % 2][0:D, t * 128:(t + 1) * 128], ones_bf[:, :], tie[:, t, :], start=False,
                                  stop=t == ST - 1, skip_group_check=True)
                    last.then_inc(s_fill[k % 2], 1)
                elif name == "ffn_up":
                    for i in range(2):
                        fill(f"up{i}", v, 128, [(w64c("ffn_w1")[:, i * 128:(i + 1) * 128], xn[:, b, 1:SEQ + 1])])
                elif name == "ffn_down":
                    evacuated(pe, "up0", v)
                    evacuated(pe, "up1", v)
                    w2 = w128c("ffn_w2")
                    fill("y", v, D, [(w2[:, i * D:(i + 1) * D], ffh[:, i, :]) for i in range(2)])

            def replicate(c):
                v, p = divmod(c, P_DIM)
                g, l = divmod(p, PL)
                for q, (rep, made, used) in enumerate(((dt_rep, s_dtrep, s_decay), (dx_rep, s_dxrep, s_drive))):
                    if p == 0 and q == 0:
                        pe.wait_ge(s_stack[v % 2], 16 * SPLITS * G * (v // 2 + 1))
                    if c >= 2:
                        pe.wait_ge(used, c - 1)
                    mm(rep[c % 2][:, :], sel_bf[:, l, :], stack[0:SPLITS * 32, q, v % 2, g, :], start=True, stop=True)\
                        .then_inc(made, 1)

            def sum_n(c):
                v, p = divmod(c, P_DIM)
                g, l = divmod(p, PL)
                if p == 0 and v >= 2:
                    pe.wait_ge(S["gate"], v - 1)
                pe.wait_ge(s_hc, c + 1)
                mm(y_ps[v % 2][32 * g:32 * g + 32, :], ssum[:, l, :], hc[:, c % RC, :], start=l == 0, stop=l == PL - 1,
                   tile_position=(0, 32 * g)).then_inc(s_ysum, 1)

            for u, s in SLOTS:
                for name, v in PLAN.get((u, s), []):
                    small(name, v)
                if 0 <= u < UNITS:
                    c = u * P_DIM + s
                    replicate(c)
                    if c >= LAG:
                        sum_n(c - LAG)
                    if c == UNITS * P_DIM - 1:
                        for k in range(c - LAG + 1, c + 1):
                            sum_n(k)

        @block.vector
        def _(ve):
            v_ = nc.vector
            chain = [0]

            def link(ins):
                chain[0] += 1
                ins.then_inc(s_dve, 1)
                ve.wait_ge(s_dve, chain[0])

            half = K1 // 2
            v_.memset(hot[:, :, 0:half], 0.0)
            v_.memset(hot[:, :, SEQ + half - 1:SEQ + K1 - 1], 0.0)
            v_.memset(hid1[:, :, 0:2], 0.0)
            v_.memset(hid1[:, :, SEQ + 2:SEQ + 4], 0.0)
            v_.memset(hid2[:, :, 0:1], 0.0)
            v_.memset(hid2[:, :, SEQ + 1:SEQ + 2], 0.0)
            v_.memset(xn[:, :, 0:1], 0.0)
            v_.memset(ones_bf[:, :], 1.0)
            v_.memset(xn[:, :, SEQ + 1:SEQ + 2], 0.0).then_inc(s_pad, 1)
            ve.wait_ge(s_load[2], 16)
            ve.wait_ge(s_firsthi, 1)
            link(v_.tensor_tensor(first_rest[:, 0, :], first, first_split[:, 0, :], ALU.subtract))
            link(v_.tensor_copy(first_split[:, 1, :], first_rest[:, 0, :]))
            v_.tensor_tensor(first_split[:, 2, :], first_rest[:, 0, :], first_split[:, 1, :], ALU.subtract).then_inc(s_first, 1)
            ve.wait_ge(s_load[0], 16)
            ve.wait_ge(s_load[3], 16)
            ve.wait_ge(s_pad, 1)
            for b in range(BATCH):
                for i in range(2):
                    rows = slice(VOCAB * i, VOCAB * i + VOCAB)
                    v_.tensor_scalar(hot[rows, b, half - i:half - i + SEQ], ids_sb[rows, b, :], constc("vocab")[rows, :], None,
                                     ALU.is_equal).then_inc(s_hot, 1)
            for k in range(3):
                n = min(6, TILES - 6 * k)
                ve.wait_ge(s_gather, 6 * k + n)
                last = v_.tensor_copy(loc[:, 6 * k:6 * k + n, :], gathered[k][:, 0:n * (D + 4)].rearrange("p (j e) -> p j e", j=n))
            link(last)

            def over_scales(a):
                return a.unsqueeze(2).to_broadcast([128, TILES, SCALES])

            def over_tiles(a):
                return a.unsqueeze(1).to_broadcast([128, TILES, SCALES])

            lshift, lwidth, lamp, lphase = (loc[:, :, D + k] for k in range(4))
            v_.scalar_tensor_tensor(center[:, :], lshift, 0.05, constc("place"), ALU.mult, ALU.add)
            v_.tensor_scalar(phase[:, :], lphase, 0.5, 0.25, ALU.mult, ALU.add)
            link(v_.scalar_tensor_tensor(absw[:, :], lwidth, -1.0, lwidth, ALU.mult, ALU.max))
            link(v_.tensor_tensor(width[:, :, :], over_scales(absw[:, :]), over_tiles(w128c("widths")), ALU.mult))
            link(v_.tensor_scalar(width[:, :, :], width[:, :, :], 1e-5, None, ALU.add))
            link(v_.reciprocal(inv_w[:, :, :], width[:, :, :]))
            v_.scalar_tensor_tensor(neg_half[:, :, :], inv_w[:, :, :], -0.5, inv_w[:, :, :], ALU.mult, ALU.mult).then_inc(s_param, 1)
            v_.tensor_scalar(neg_b3[:, :], w128c("b3"), -1.0, None, ALU.mult).then_inc(s_negb3, 1)
            for d in range(2):
                last = v_.tensor_tensor(dt_b[:, d:d + 1], w128c("fb"[d] + "_xp_bdt"), w128c("fb"[d] + "_dt_bias"), ALU.add)
            last.then_inc(S["bias"], 1)
            link(v_.tensor_tensor(sw2[:, :], w128c("sw"), w128c("sw"), ALU.mult))
            ve.wait_ge(s_ampexp, 1)
            link(v_.tensor_scalar(amp_den[:, :], amp_exp[:, :], 1.0, None, ALU.add))
            link(v_.reciprocal(amp_scale[:, :], amp_den[:, :]))
            link(v_.tensor_tensor(scale_w[:, :, :], over_scales(amp_scale[:, :]), over_tiles(sw2[:, :]), ALU.mult))

            ve.wait_ge(s_load[4], 16)

            def amplitudes():
                ve.wait_ge(s_ctxexp, 1)
                link(v_.tensor_scalar(ctx_den[:, :], ctx_exp[:, :], 1.0, None, ALU.add))
                link(v_.reciprocal(ctx_sig[:, :], ctx_den[:, :]))
                link(v_.tensor_tensor(ctx_w[:, :, :], over_scales(ctx_sig[:, :]), scale_w[:, :, :], ALU.mult))
                for b in range(BATCH):
                    js = slice(b * ST, (b + 1) * ST)
                    v_.tensor_tensor(amps[:, js, :, :], loc[:, js, 0:D].unsqueeze(2).to_broadcast([128, ST, SCALES, D]),
                                     ctx_w[:, js, :].unsqueeze(3).to_broadcast([128, ST, SCALES, D]), ALU.mult).then_inc(s_amps, 1)

            for j in range(TILES):
                b = j // ST
                if j >= RX:
                    ve.wait_ge(s_xd2, j - RX + 1)
                if j >= RT:
                    ve.wait_ge(s_wave, j - RT + 1)
                v_.tensor_scalar(xd[:, j % RX, :], pos_sb[:, b, :], center[:, j:j + 1], None, ALU.subtract).then_inc(s_xd, 1)
                ve.wait_ge(s_xd, j + 1)
                for s in range(SCALES):
                    last = v_.tensor_scalar(turn[:, j % RT, s, :], xd[:, j % RX, :], inv_w[:, j, s:s + 1], phase[:, j:j + 1],
                                            ALU.mult, ALU.add)
                link(last)
                link(v_.tensor_scalar(nearest[:, :, :], turn[:, j % RT, :, :], ROUND, -ROUND, ALU.add, ALU.add))
                v_.tensor_tensor(turn[:, j % RT, :, :], turn[:, j % RT, :, :], nearest[:, :, :], ALU.subtract).then_inc(s_turn, 1)
                ve.wait_ge(s_turn, j + 1)
                if j == RT:
                    amplitudes()

            ve.wait_ge(s_field, TILES)
            ve.wait_ge(s_sin, TILES)
            v_.memset(decay[:, :, 0:1], 0.0).then_inc(S["A"], 1)
            v_.tensor_copy(sel_bf[:, :, :], sel[0:SPLITS * 32, :, :]).then_inc(S["sel"], 1)
            for k in range(KD):
                last = v_.tensor_scalar(diag[:, k, :], constc("eye")[0:D, :], w64c("conv_w", k), None, ALU.mult)
            last.then_inc(S["diag"], 1)

            def read(product, v):
                k = FILL[product, v]
                filled(ve, product, v)
                return shared[k % 2], s_evac[k % 2]

            def small(name, v):
                d, b = divmod(v, BATCH)
                D_ = "fb"[d]
                if name == "ln1_center":
                    ps, ev = read("m1", v)
                    if b:
                        ve.wait_ge(S["xn"], b)
                    v_.tensor_tensor(ln_a[:, 0, :], h1[:, b, :], ps[0:D, :], ALU.subtract).then_inc(ev, 1)
                elif name == "dt_sum":
                    ve.wait_ge(S["sp_parts"], v + 1)
                    if v:
                        ve.wait_ge(S["rest"], 2 * v)
                    link(v_.tensor_scalar(sp2[:, 0, :], sp[:, 0, :], 1.0, -1.0, ALU.add, ALU.add))
                    link(v_.tensor_tensor(sp2[:, 0, :], sp2[:, 0, :], sp[:, 0, :], ALU.subtract))
                    link(v_.tensor_tensor(sp2[:, 0, :], sp[:, 2, :], sp2[:, 0, :], ALU.subtract))
                    v_.tensor_tensor(dt[:, 0, :], sp2[:, 0, :], sp[:, 1, :], ALU.add).then_inc(S["dt"], 1)
                    ve.wait_ge(S["dt"], v + 1)
                    v_.tensor_tensor(dtx[:, 0, :], dt[:, 0, :], xi[:, v % 2, :], ALU.mult).then_inc(S["dtx"], 1)
                elif name == "gate":
                    if v:
                        filled(ve, "o", v - 1)
                    ve.wait_ge(s_ysum, P_DIM * (v + 1))
                    link(v_.scalar_tensor_tensor(gated[:, 0, :], xi[:, v % 2, :], w128c(D_ + "_D_skip"), y_ps[v % 2][:, :],
                                                 ALU.mult, ALU.add))
                    v_.tensor_tensor(gated[:, 0, :], gated[:, 0, :], zs[:, v % 2, :], ALU.mult).then_inc(S["gate"], 1)
                elif name == "ln2_center":
                    ps, ev = read("m2", v)
                    v_.tensor_tensor(ln_a[:, 1, :], ln_a[:, 1, :], ps[0:D, :], ALU.subtract).then_inc(ev, 1)
                elif name == "ln2_scale":
                    ve.wait_ge(S["rstd2"], b + 1)
                    v_.scalar_tensor_tensor(ln_b[:, 1, :], ln_a[:, 1, :], w64c("norm_w"), ln_b[:, 3, :], ALU.mult, ALU.mult)\
                        .then_inc(S["sc2"], 1)
                elif name == "h2":
                    ps, ev = read("o", v)
                    ve.wait_ge(S["cgelu"], 1)
                    link(v_.tensor_tensor(ln_a[:, 3, :], h1[:, b, :], hacc[:, b, :], ALU.add))
                    v_.scalar_tensor_tensor(h1[:, b, :], ps[0:D, ::-1], w64c("b_out_b"), ln_a[:, 3, :], ALU.add, ALU.add)\
                        .then_inc(ev, 1)
                elif name == "ln3_center":
                    ps, ev = read("m3", v)
                    v_.tensor_tensor(ln_a[:, 2, :], h1[:, b, :], ps[0:D, :], ALU.subtract).then_inc(ev, 1)
                elif name == "ln3_out":
                    ve.wait_ge(S["rstd3"], b + 1)
                    link(v_.tensor_tensor(xn[:, b, 1:SEQ + 1], ln_a[:, 2, :], ln_b[:, 3, :], ALU.mult))
                    v_.tensor_tensor(h1[:, b, :], h1[:, b, :], xn[:, b, 1:SEQ + 1], ALU.add).then_inc(S["xn3"], 1)
                elif name == "ffn_route_copy":
                    ps, ev = read("w", v)
                    v_.tensor_scalar(wrow[:, 0, :], ps[:, :], w128c("br"), None, ALU.add).then_inc(ev, 1)
                elif name == "ffn_col_copy":
                    ps, ev = read("wc", v)
                    v_.tensor_copy(wcol[:, :], ps[:, 0:ST]).then_inc(ev, 1)
                elif name == "ffn_mask":
                    ps, ev = read("rank", v)
                    v_.scalar_tensor_tensor(mask[:, :], ps[0:D, :], CAP - 0.5, wrow[0:D, 0, :], ALU.is_lt, ALU.mult).then_inc(ev, 1)
                elif name == "ffn_rank":
                    evacuated(ve, "w", v)
                    evacuated(ve, "wc", v)
                    for t in range(ST):
                        here = slice(t * 128, (t + 1) * 128)
                        v_.tensor_scalar(bits[t][:, 0:(t + 1) * 128], wrow[:, 0, 0:(t + 1) * 128], wcol[:, t:t + 1], None, ALU.is_lt)
                        if t + 1 < ST:
                            v_.tensor_scalar(bits[t][:, (t + 1) * 128:], wrow[:, 0, (t + 1) * 128:], wcol[:, t:t + 1], None, ALU.is_le)
                        last = v_.scalar_tensor_tensor(tie[:, t, :], wrow[:, 0, here], wcol[:, t:t + 1], constc("tri"),
                                                       ALU.is_equal, ALU.mult)
                    last.then_inc(S["rankbits"], 1)
                elif name == "ffn_out":
                    ps, ev = read("y", v)
                    if b >= 2:
                        ve.wait_ge(s_outdma[b % 2], 16 * (b // 2))
                    evacuated(ve, "rank", v)
                    v_.scalar_tensor_tensor(ffin[:, b % 2, :], ps[0:D, :], w64c("ffn_b2"), mask[:, :], ALU.add, ALU.mult)\
                        .then_inc(ev, 1)
                    evacuated(ve, "y", v)
                    v_.tensor_tensor(ffin[:, b % 2, :], ffin[:, b % 2, :], h1[:, b, :], ALU.add).then_inc(S["out"], 1)

            def drive_step(c):
                v = c // P_DIM
                if c % P_DIM == 0:
                    evacuated(ve, "B", v)
                ve.wait_ge(s_dxrep, c + 1)
                v_.tensor_tensor(drive[:, c % RC, :], dx_rep[c % 2][:, :], Bt[:, v % 2, :], ALU.mult).then_inc(s_drive, 1)

            def scan_step(c):
                ve.wait_ge(s_decay, c + 1)
                ve.wait_ge(s_drive, c + 1)
                if c >= RC:
                    ve.wait_ge(s_hc, c - RC + 1)
                v_.tensor_tensor_scan(state[:, c % RC, :], decay[:, c % RC, :], drive[:, c % RC, :], 0.0,
                                      ALU.mult, ALU.add).then_inc(s_state, 1)

            for u, s in SLOTS:
                for name, v in PLAN.get((u, s), []):
                    small(name, v)
                if 0 <= u < UNITS:
                    c = u * P_DIM + s
                    drive_step(c)
                    if c >= 1:
                        scan_step(c - 1)
                    if c == UNITS * P_DIM - 1:
                        scan_step(c)

        @block.scalar
        def _(ac):
            act = nc.scalar.activation
            chain = [0]

            def link(ins):
                chain[0] += 1
                ins.then_inc(s_act, 1)
                ac.wait_ge(s_act, chain[0])

            ac.wait_ge(s_load[2], 16)
            act(first_split[:, 0, :], first, ACT.Copy).then_inc(s_firsthi, 1)
            ac.wait_ge(s_load[3], 16)
            for d in range(2):
                last = act(neg_A[:, d, :], w128c("fb"[d] + "_A_log"), ACT.Exp)
            link(last)
            link(act(neg_A[:, :, :], neg_A[:, :, :], ACT.Copy, scale=-1.0))
            ac.wait_ge(s_param, 1)
            act(amp_exp[:, :], loc[:, :, D + 2], ACT.Exp, scale=-1.0).then_inc(s_ampexp, 1)
            ac.wait_ge(s_negb3, 1)

            def hidden1(b):
                ac.wait_ge(s_conv1, b + 1)
                act(hid1[:, b, 2:2 + SEQ], conv_ps[b][:, :], ACT.Gelu, bias=w128c("tok_b1")).then_inc(s_hid1, 1)

            def hidden2(b):
                ac.wait_ge(s_conv2, b + 1)
                act(hid2[:, b, 1:1 + SEQ], conv_ps[b][0:D, :], ACT.Gelu, bias=w64c("b2")).then_inc(s_hid2, 1)

            def envelopes(b):
                for j in range(b * ST, (b + 1) * ST):
                    ac.wait_ge(s_xd, j + 1)
                    if j >= 2:
                        ac.wait_ge(s_env, j - 1)
                    act(xd2[:, j % 2, :], xd[:, j % RX, :], ACT.Square).then_inc(s_xd2, 1)
                    ac.wait_ge(s_xd2, j + 1)
                    if j >= RE:
                        ac.wait_ge(s_field, j - RE + 1)
                    for s in range(SCALES):
                        last = act(env[:, j % RE, s, :], xd2[:, j % 2, :], ACT.Exp, scale=neg_half[:, j, s:s + 1])
                    last.then_inc(s_env, 1)

            def waves(b):
                for j in range(b * ST, (b + 1) * ST):
                    ac.wait_ge(s_turn, j + 1)
                    act(turn[:, j % RT, :, :], turn[:, j % RT, :, :], ACT.Sin, scale=TWO_PI).then_inc(s_sin, 1)

            def field_out(b):
                ac.wait_ge(s_field, ST * (b + 1))
                act(h1[:, b, :], field_ps[b % 2][0:D, :], ACT.Copy).then_inc(s_h1, 1)

            envelopes(0)
            for b in range(BATCH):
                hidden1(b)
            waves(0)
            ac.wait_ge(s_load[1], 16)
            for b in range(BATCH):
                hidden2(b)
            ac.wait_ge(s_conv3, BATCH)
            act(ctx_exp[:, :], ctx_logit[:, 0:TILES], ACT.Exp, bias=neg_b3[:, :], scale=-1.0).then_inc(s_ctxexp, 1)
            envelopes(1)
            waves(1)
            envelopes(2)
            field_out(0)
            waves(2)
            envelopes(3)
            field_out(1)
            waves(3)
            nc.scalar.preload_act_table_set("natural_log_exp_and_others")
            field_out(2)
            field_out(3)
            ac.wait_ge(S["A"], 1)
            ac.wait_ge(S["bias"], 1)

            def read(product, v):
                k = FILL[product, v]
                filled(ac, product, v)
                return shared[k % 2], s_evac[k % 2]

            def rstd(product, v, out_):
                ps, ev = read(product, v)
                act(out_, ps[0:D, :], ACT.Ln, bias=constc("eps")[0:D, :]).then_inc(ev, 1)
                evacuated(ac, product, v)

            def small(name, v):
                d, b = divmod(v, BATCH)
                D_ = "fb"[d]
                if name == "ln1_square":
                    evacuated(ac, "m1", v)
                    act(ln_b[:, 0, :], ln_a[:, 0, :], ACT.Square).then_inc(S["sq1"], 1)
                elif name == "ln1_rstd":
                    rstd("v1", v, ln_b[:, 2, :])
                    act(ln_b[:, 2, :], ln_b[:, 2, :], ACT.Exp, scale=-0.5).then_inc(S["rstd1"], 1)
                elif name == "silu":
                    if v >= 2:
                        ac.wait_ge(S["gate"], v - 1)
                    for product, bias, to in (("xi", "_in_bx", xi), ("z", "_in_bz", zs)):
                        ps, ev = read(product, v)
                        act(to[:, v % 2, :], ps[:, :], ACT.Silu, bias=w128c(D_ + bias)).then_inc(ev, 1)
                    nc.scalar.preload_act_table_set("natural_log_exp_and_others")
                elif name == "softplus":
                    ps, ev = read("dt", v)
                    if v:
                        ac.wait_ge(S["dt"], v)
                    link(act(sp[:, 0, :], ps[:, :], ACT.Abs, bias=dt_b[:, d:d + 1]))
                    act(sp[:, 1, :], ps[:, :], ACT.Relu, bias=dt_b[:, d:d + 1]).then_inc(ev, 1)
                    link(act(sp[:, 0, :], sp[:, 0, :], ACT.Exp, scale=-1.0))
                    act(sp[:, 2, :], sp[:, 0, :], ACT.Ln, bias=constc("one")).then_inc(S["sp_parts"], 1)
                    ps, ev = read("B", v)
                    if v >= 2:
                        ac.wait_ge(s_drive, P_DIM * (v - 1))
                    act(Bt[:, v % 2, :], ps[:, :], ACT.Identity, bias=w128c(D_ + "_xp_bB")).then_inc(ev, 1)
                elif name == "split_hi":
                    for q, x in enumerate((dt, dtx)):
                        ac.wait_ge(S[("dt", "dtx")[q]], v + 1)
                        if v:
                            ac.wait_ge(s_stack[(v - 1) % 2], 16 * SPLITS * G * ((v - 1) // 2 + 1))
                        act(part[:, q, 0, :], x[:, 0, :], ACT.Copy).then_inc(S["hi"], 1)
                    ps, ev = read("C", v)
                    if v >= 2:
                        ac.wait_ge(s_hc, P_DIM * (v - 1))
                    act(Ct[:, v % 2, :], ps[:, :], ACT.Identity, bias=w128c(D_ + "_xp_bC")).then_inc(ev, 1)
                elif name == "split_mid":
                    for q in range(2):
                        ac.wait_ge(S["rest"], 2 * v + q + 1)
                        act(part[:, q, 1, :], rest[:, q, :], ACT.Copy).then_inc(S["mid"], 1)
                elif name == "conv_out":
                    ps, ev = read("cv", v)
                    act(hacc[:, b, :], ps[0:D, :], ACT.Copy).then_inc(ev, 1)
                elif name == "out_bias":
                    ps, ev = read("o", v)
                    if b:
                        ac.wait_ge(S["sc2"], b)
                    act(ln_a[:, 1, :], ps[0:D, :], ACT.Identity, bias=w64c("f_out_b")).then_inc(ev, 1)
                elif name == "ln2_square":
                    evacuated(ac, "m2", v)
                    act(ln_b[:, 1, :], ln_a[:, 1, :], ACT.Square).then_inc(S["sq2"], 1)
                elif name == "ln2_rstd":
                    rstd("v2", v, ln_b[:, 3, :])
                    act(ln_b[:, 3, :], ln_b[:, 3, :], ACT.Exp, scale=-0.5).then_inc(S["rstd2"], 1)
                elif name == "ln2_out":
                    ac.wait_ge(S["sc2"], b + 1)
                    act(y1n[:, b, ::-1], ln_b[:, 1, :], ACT.Identity, bias=w64c("norm_b")).then_inc(S["y1n"], 1)
                elif name == "ln3_square":
                    evacuated(ac, "m3", v)
                    act(ln_b[:, 1, :], ln_a[:, 2, :], ACT.Square).then_inc(S["sq3"], 1)
                elif name == "ln3_rstd":
                    if b:
                        ac.wait_ge(S["xn3"], b)
                    rstd("v3", v, ln_b[:, 3, :])
                    act(ln_b[:, 3, :], ln_b[:, 3, :], ACT.Exp, scale=-0.5).then_inc(S["rstd3"], 1)
                elif name == "conv_gelu":
                    evacuated(ac, "cv", BATCH - 1)
                    act(hacc[:, :, :], hacc[:, :, :], ACT.Gelu, bias=w64c("conv_b")).then_inc(S["cgelu"], 1)
                    nc.scalar.preload_act_table_set("natural_log_exp_and_others")
                elif name == "ffn_gelu":
                    if b:
                        filled(ac, "y", v - 1)
                    for i in range(2):
                        ps, ev = read(f"up{i}", v)
                        act(ffh[:, i, :], ps[:, :], ACT.Gelu_apprx_tanh, bias=w128c("ffn_b1", i)).then_inc(ev, 1)
                    nc.scalar.preload_act_table_set("natural_log_exp_and_others")

            def decay_step(c):
                d, p = c // P_DIM // BATCH, c % P_DIM
                ac.wait_ge(s_dtrep, c + 1)
                if c >= RC:
                    ac.wait_ge(s_state, c - RC + 1)
                act(decay[:, c % RC, 1:], dt_rep[c % 2][:, 1:], ACT.Exp, scale=neg_A[:, d, p:p + 1]).then_inc(s_decay, 1)

            for u, s in SLOTS:
                for name, v in PLAN.get((u, s), []):
                    small(name, v)
                if 0 <= u < UNITS:
                    decay_step(u * P_DIM + s)

        @block.gpsimd
        def _(po):
            tt = nc.gpsimd.tensor_tensor
            for j in range(TILES):
                po.wait_ge(s_env, j + 1)
                po.wait_ge(s_sin, j + 1)
                tt(env[:, j % RE, :, :], env[:, j % RE, :, :], turn[:, j % RT, :, :], ALU.mult).then_inc(s_wave, 1)

            def small(name, v):
                d, b = divmod(v, BATCH)
                if name == "ln1_out":
                    po.wait_ge(S["rstd1"], b + 1)
                    tt(xn[:, b, 1:SEQ + 1], ln_a[:, 0, :], ln_b[:, 2, :], ALU.mult).then_inc(S["xn"], 1)
                elif name == "split_rest":
                    for q, x in enumerate((dt, dtx)):
                        po.wait_ge(S["hi"], 2 * v + q + 1)
                        if v:
                            po.wait_ge(S["lo"], 2 * v)
                        tt(rest[:, q, :], x[:, 0, :], part[:, q, 0, :], ALU.subtract).then_inc(S["rest"], 1)
                elif name == "split_lo":
                    for q in range(2):
                        po.wait_ge(S["mid"], 2 * v + q + 1)
                        tt(part[:, q, 2, :], rest[:, q, :], part[:, q, 1, :], ALU.subtract).then_inc(S["lo"], 1)

            def read_out(c):
                v = c // P_DIM
                if c % P_DIM == 0:
                    evacuated(po, "C", v)
                po.wait_ge(s_state, c + 1)
                if c >= RC:
                    po.wait_ge(s_ysum, c - RC + 1)
                tt(hc[:, c % RC, :], state[:, c % RC, :], Ct[:, v % 2, :], ALU.mult).then_inc(s_hc, 1)

            for u, s in SLOTS:
                for name, v in PLAN.get((u, s), []):
                    small(name, v)
                if 0 <= u < UNITS:
                    read_out(u * P_DIM + s)


def constants():
    c = {}
    r = np.arange(128)
    h_r, l_r = r % 32 // PL, r % PL
    c["sel"] = ((l_r[:, None, None] == np.arange(PL)[None, :, None])
                & (h_r[:, None, None] == (r // N_DIM)[None, None, :])).reshape(128, -1)
    q = np.arange(32)
    c["ssum"] = (((r // N_DIM)[:, None, None] == (q // PL)[None, None, :])
                 & (np.arange(PL)[None, :, None] == (q % PL)[None, None, :])).reshape(128, -1)
    c["tri"] = r[:, None] < r[None, :]
    line = (np.arange(SEQ, dtype=np.float32) / np.float32(SEQ - 1)).astype(np.float32)
    c["place"] = np.tile(line.reshape(ST, 128).T, (1, BATCH))
    c["eps"] = np.full((128, 1), LN_EPS)
    c["one"] = np.ones((128, 1))
    c["mean"] = np.full((128, D), 1.0 / D)
    c["eye"] = np.eye(128, D)
    c["vocab"] = r[:, None] % VOCAB
    out = np.zeros((128, C128_N), np.float32)
    for name, (a, b) in C128.items():
        out[:, a:b] = c[name]
    return out


def kernel(**inputs):
    import concourse.bacc as bacc
    from concourse.bass_utils import run_bass_kernel_spmd

    x = {k: np.asarray(v) for k, v in inputs.items()}
    perm = np.arange(DI).reshape(HEADS, G, PL).transpose(1, 0, 2).reshape(-1)

    def row(a, p=128):
        return np.broadcast_to(a.reshape(1, -1), (p, a.size))

    w1 = np.zeros((2, VOCAB, PAIRS, HID), np.float32)
    for k in range(K1):
        w1[k % 2, :, k // 2, :] = x["L0_tok_w1"][:, :, k].T
    embloc = np.zeros((128, D + 4), np.float32)
    embloc[:VOCAB] = np.concatenate([x["L0_tok_emb"], x["L0_tok_locality_shapes"]], 1)
    p128 = {
        "tok_w1": w1.reshape(128, -1), "embloc": embloc,
        "tok_w2": x["L0_tok_w2"].transpose(1, 2, 0).reshape(HID, -1), "tok_b1": x["L0_tok_b1"][:, None],
        "b3": row(x["L0_tok_b3"]), "widths": row(x["L0_tok_multiscale_widths"]), "sw": row(x["L0_tok_scale_weights"]),
        "br": row(x["L0_ffn_br"]),
        "ffn_w2": x["L0_ffn_w2"].reshape(2, 128, D).transpose(1, 0, 2).reshape(128, -1),
        "ffn_b1": x["L0_ffn_b1"].reshape(2, 128).T,
    }
    p64 = {
        "w3": x["L0_tok_w3"][0], "b2": x["L0_tok_b2"][:, None],
        "norm_w": x["L0_attn_norm_w"][:, None], "norm_b": x["L0_attn_norm_b"][:, None],
        "conv_w": x["L0_attn_conv_w"][:, 0, :], "conv_b": x["L0_attn_conv_b"][:, None],
        "ffn_w1": x["L0_ffn_w1"], "wr": np.broadcast_to(x["L0_ffn_wr"], (D, 128)), "ffn_b2": x["L0_ffn_b2"][:, None],
    }
    for d in "fb":
        g = {k[len("L0_attn_f_"):]: v for k, v in x.items() if k.startswith(f"L0_attn_{d}_")}
        xp, xb = g["x_proj_w"][:, perm], g["x_proj_b"][:, None]
        p128 |= {
            f"{d}_xp_dt": xp[:DI][perm].T, f"{d}_xp_B": xp[DI:2 * DI].T, f"{d}_xp_C": xp[2 * DI:].T,
            f"{d}_in_bx": g["in_proj_b"][:DI][perm][:, None], f"{d}_in_bz": g["in_proj_b"][DI:][perm][:, None],
            f"{d}_xp_bdt": xb[:DI][perm], f"{d}_dt_bias": g["dt_bias"][perm][:, None],
            f"{d}_xp_bB": xb[DI:2 * DI], f"{d}_xp_bC": xb[2 * DI:], f"{d}_D_skip": g["D_skip"][perm][:, None],
            f"{d}_A_log": g["A_log"].reshape(HEADS, P_DIM, N_DIM).transpose(0, 2, 1).reshape(128, P_DIM),
            f"{d}_out_w": g["out_proj_w"][:, perm].T,
        }
        p64 |= {f"{d}_in_wx": g["in_proj_w"][:DI][perm].T, f"{d}_in_wz": g["in_proj_w"][DI:][perm].T,
                f"{d}_out_b": g["out_proj_b"][:, None]}

    def side_by_side(parts, places):
        return np.ascontiguousarray(np.concatenate([parts[n] for n in places], 1))

    arrays = {
        "ids": np.ascontiguousarray(np.broadcast_to(x["x"], (128, BATCH, SEQ))),
        "w64": side_by_side(p64, W64), "w128": side_by_side(p128, W128),
        "pos": np.ascontiguousarray(np.broadcast_to(x["fside_BS_continuous_positions"], (128, BATCH, SEQ))),
        "const": constants(),
    }
    nc = bacc.Bacc("TRN2", target_bir_lowering=False, num_devices=1)
    args = [nc.dram_tensor(n, a.shape, mybir.dt.from_np(a.dtype), kind="ExternalInput").ap() for n, a in arrays.items()]
    out = nc.dram_tensor("out", (D, BATCH, SEQ), F32, kind="ExternalOutput").ap()
    build(nc, *args, out)
    r = run_bass_kernel_spmd(nc, [arrays], core_ids=[0])
    return r.results[0]["out"].transpose(1, 2, 0)
```

```python
from contextlib import ExitStack

import numpy as np

import concourse.bass as bass
from concourse import mybir

ALU = mybir.AluOpType
ACT = mybir.ActivationFunctionType
F32 = mybir.dt.float32
BF16 = mybir.dt.bfloat16
I32 = mybir.dt.int32

BATCH, SEQ, D = 4, 512, 64
VOCAB = 64
HID = 128
K1, K2, K3 = 7, 5, 3
KD = 3
SCALES = 4
ST = SEQ // 128
TILES = BATCH * ST
DI, HEADS, P_DIM, N_DIM = 128, 8, 16, 16
G = 4
PL = P_DIM // G
FF = 256
CAP = SEQ // 2 - 1
UNITS = 2 * BATCH
LN_EPS = 1e-5
ROUND = 1.5 * 2.0 ** 23
TWO_PI = 6.283185

RE = 6
RT = 6
RX = 5
EARLY = 16
SPLITS = 3
PAIRS = (K1 + 1) // 2
FIRST = PAIRS * HID + D + 4
RC = 6
RD = 8
RS = 8
RH = 8
LEAD_DT, LEAD_DECAY, LEAD_DX = 3, 2, 2
LAG = 5


def columns(parts):
    at, out = 0, {}
    for name, n in parts:
        out[name] = (at, at + n)
        at += n
    return out, at


W128, W128_N = columns(
    [("tok_w1", PAIRS * HID), ("embloc", D + 4), ("tok_w2", K2 * D), ("tok_b1", 1), ("b3", 1), ("widths", SCALES), ("sw", SCALES), ("br", 1),
     ("ffn_w2", 2 * D), ("ffn_b1", 2)]
    + [(f"{d}_{n}", k) for d in "fb" for n, k in
       (("xp_dt", DI), ("xp_B", DI), ("xp_C", DI), ("in_bx", 1), ("in_bz", 1), ("xp_bdt", 1), ("dt_bias", 1),
        ("xp_bB", 1), ("xp_bC", 1), ("D_skip", 1), ("A_log", P_DIM), ("out_w", D))])
W64, W64_N = columns(
    [("w3", K3), ("b2", 1), ("norm_w", 1), ("norm_b", 1),
     ("conv_w", KD), ("conv_b", 1), ("ffn_w1", FF), ("wr", 128), ("ffn_b2", 1)]
    + [(f"{d}_{n}", k) for d in "fb" for n, k in (("in_wx", DI), ("in_wz", DI), ("out_b", 1))])
C128, C128_N = columns(
    [("sel", PL * 128), ("ssum", PL * 32), ("tri", 128), ("place", TILES), ("eps", 1), ("one", 1), ("mean", D), ("centering", D),
     ("eye", D), ("vocab", 1)])


def make_plan():
    plan = {}

    def steps(v, u, s, *which):
        for k, n in which:
            at = (u + (s + k) // P_DIM, (s + k) % P_DIM) if 0 <= u < UNITS else (u, s + k)
            plan.setdefault(at, []).append((n, v))

    ln1 = ((0, "ln1_center"), (1, "ln1_square"), (2, "ln1_var"), (3, "ln1_rstd"), (4, "ln1_out"))
    front_in = ((0, "in_proj_x"), (1, "in_proj_z"))
    front = ((0, "silu"), (1, "x_proj_dt"), (2, "x_proj_B"), (2, "softplus_arg"), (3, "softplus_log"), (3, "x_proj_C"),
             (4, "C_out"), (3, "dt_log1p"), (3, "dt_out"), (4, "dtx_out"), (4, "dt_parts"), (5, "dtx_parts"))
    post_f = ((0, "gate"), (3, "out_proj"), (4, "ln2_square"), (5, "ln2_var"), (6, "ln2_rstd"), (7, "ln2_scale"),
              (10, "ln2_out"))
    post_b = ((0, "gate"), (3, "out_proj"), (4, "h2"), (7, "ln3_center"), (8, "ln3_square"), (9, "ln3_var"),
              (10, "ln3_rstd"), (10, "ln3_out"), (11, "residual"))
    ffn = ((0, "ffn_route"), (1, "ffn_route_copy"), (2, "ffn_col"), (3, "ffn_col_copy"), (4, "ffn_rank0"),
           (5, "ffn_rank1"), (6, "ffn_rank2"), (7, "ffn_rank3"), (8, "ffn_up"), (9, "ffn_gelu"), (11, "ffn_rank_sum"),
           (12, "ffn_mask"), (12, "ffn_down"), (13, "ffn_out"))
    last_post = ((0, "gate"), (1, "out_proj"), (2, "h2"), (3, "ln3_center"), (4, "ln3_square"), (5, "ln3_var"),
                 (6, "ln3_rstd"), (7, "ln3_out"), (8, "residual"), (9, "ffn_route"), (10, "ffn_route_copy"),
                 (11, "ffn_col"), (12, "ffn_col_copy"), *((12, f"ffn_rank{t}") for t in range(ST)),
                 (14, "ffn_up"), (14, "ffn_gelu"),
                 (16, "ffn_rank_sum"), (16, "ffn_mask"), (17, "ffn_down"), (18, "ffn_out"))
    ffn_before = ((0, "ffn_route"), (1, "ffn_route_copy"), (2, "ffn_col"), (3, "ffn_col_copy"),
                  *((4, f"ffn_rank{t}") for t in range(ST)),
                  (4, "ffn_up"), (5, "ffn_gelu"), (6, "ffn_rank_sum"), (7, "ffn_mask"), (7, "ffn_down"), (8, "ffn_out"))

    steps(0, -1, 0, *ln1)
    steps(0, -1, 5, *front_in)
    steps(0, -1, 7, *front)
    steps(1, -1, 11, *ln1)
    steps(1, 0, 0, *front_in)
    for v in range(UNITS):
        if v + 1 < UNITS:
            steps(v + 1, v, 0 if v else 2, *front)
        if v >= 1:
            steps(v - 1, v, LAG, *(post_f if v - 1 < BATCH else post_b))
        if v + 2 < BATCH:
            steps(v + 2, v, 6, *ln1)
        if v < BATCH:
            steps(v, v, 11, (0, "conv"), (1, "conv_out"))
        if v == BATCH:
            steps(v, v, 6, (0, "conv_gelu"))
            for b in range(BATCH):
                steps(b, v + b, (9, 12, 5, 5)[b], (0, "conv_add"))
        if v - 2 >= BATCH:
            steps(v - 2, v, 3, *ffn)
        if v + 2 < UNITS:
            steps(v + 2, v, 14, *front_in)
    steps(UNITS - 1, UNITS, 0, *last_post)
    steps(UNITS - 2, UNITS, 0, *ffn_before)
    slots = [(-1, s) for s in range(EARLY)] + [(u, s) for u in range(UNITS) for s in range(P_DIM)]
    slots += [(UNITS, s) for s in range(32)]
    return plan, slots


PLAN, SLOTS = make_plan()
CORE_SLOTS = [slot for slot in SLOTS if slot[0] >= 0]


def run(kind, *tiles):
    return [(kind, t) for t in tiles]


TOKEN_ORDER = (
    run("hidden1", 0, 1) + run("amp_exponent", 0) + run("envelope", 0, 1) + run("hidden1", 2, 3) + run("wave", 0, 1)
    + run("envelope", 2, 3) + run("hidden2", 0, 1, 2, 3) + run("wave", 2, 3)
    + run("envelope", 4, 5) + run("wave", 4, 5) + run("context", 0)
    + run("envelope", 6, 7, 8) + run("wave", 6, 7, 8) + run("field_out", 0)
    + run("envelope", 9, 10) + run("slot", 1) + run("envelope", 11) + run("slot", 3)
    + run("wave", 9, 10, 11) + run("field_out", 1)
    + run("envelope", 12, 13) + run("wave", 12, 13) + run("envelope", 14, 15) + run("field_out", 2) + run("wave", 14, 15)
    + run("slot", *range(5, EARLY)) + run("field_out", 3))
SLOTS_PE = {5: range(0, 1), 7: range(1, 3), 8: range(3, 7), 13: range(7, 10), 14: range(10, 13), 15: range(13, EARLY)}
SLOTS_POOL = {8: range(0, 5), 14: range(5, EARLY)}
SLOTS_DVE = {15: range(0, EARLY)}
AMPS_AT = 6


def early(slots):
    return [step for s in slots for step in PLAN.get((-1, s), [])]


SHARED_FILLS = {"ln1_center": ["m1"], "ln1_var": ["v1"], "in_proj_x": ["xi"], "in_proj_z": ["z"], "x_proj_dt": ["dt"],
                "x_proj_B": ["B"],
                "x_proj_C": ["C"], "out_proj": ["o"], "ln2_var": ["v2"], "ln3_center": ["m3"], "ln3_var": ["v3"],
                "conv": ["cv"], "ffn_route": ["w"], "ffn_col": ["wc"], "ffn_rank_sum": ["rank"],
                "ffn_up": ["up0", "up1"], "ffn_down": ["y"]}


def number_fills():
    out, k = {}, 0
    for slot in SLOTS:
        for name, v in PLAN.get(slot, []):
            for product in SHARED_FILLS.get(name, []):
                out[product, v] = k
                k += 1
    return out


FILL = number_fills()


def build(nc, ids, w64, w128, pos, const, out):
    with ExitStack() as ctx:
        def sb(name, shape, dt=F32):
            return ctx.enter_context(nc.sbuf_tensor(name, shape, dt))

        def sem(name):
            return ctx.enter_context(nc.semaphore(name))

        bank = [ctx.enter_context(nc.psum_tensor(f"bank{i}", [128, 512], F32)) for i in range(8)]
        gathered, ctx_logit, conv_ps, field_ps = bank[0:3], bank[3], bank[4:8], bank[0:2]
        dt_rep, dx_rep, y_ps, shared = bank[0:2], bank[2:4], bank[4:6], bank[6:8]

        ids_sb = sb("ids_sb", [128, BATCH, SEQ], I32)
        w64_sb = sb("w64_sb", [64, W64_N])
        w128_sb = sb("w128_sb", [128, W128_N])
        const_sb = sb("const_sb", [128, C128_N])
        pos_sb = sb("pos_sb", [128, BATCH, SEQ])

        def w64c(name, k=None):
            a, b = W64[name]
            return w64_sb[:, a:b] if k is None else w64_sb[:, a + k:a + k + 1]

        def w128c(name, k=None):
            a, b = W128[name]
            return w128_sb[:, a:b] if k is None else w128_sb[:, a + k:a + k + 1]

        def constc(name):
            a, b = C128[name]
            return const_sb[:, a:b]

        tok_w2 = w128c("tok_w2").rearrange("c (k o) -> c k o", k=K2)
        sel = constc("sel").rearrange("r (l n) -> r l n", l=PL)
        ssum = constc("ssum").rearrange("r (l n) -> r l n", l=PL)
        mean64 = constc("mean")[0:D, :]
        centering = constc("centering")[0:D, :]

        hot = sb("hot", [128, BATCH, SEQ + K1 - 1], BF16)
        first = w128_sb[:, 0:FIRST]
        first_rest = sb("first_rest", [128, 2, FIRST])
        first_split = sb("first_split", [128, SPLITS, FIRST], BF16)
        loc = sb("loc", [128, TILES, D + 4])
        center = sb("center", [128, TILES])
        absw = sb("absw", [128, TILES])
        phase = sb("phase", [128, TILES])
        width = sb("width", [128, TILES, SCALES])
        inv_w = sb("inv_w", [128, TILES, SCALES])
        neg_half = sb("neg_half", [128, TILES, SCALES])
        amp_exp = sb("amp_exp", [128, TILES])
        amp_den = sb("amp_den", [128, TILES])
        amp_scale = sb("amp_scale", [128, TILES])
        sw2 = sb("sw2", [128, SCALES])
        scale_w = sb("scale_w", [128, TILES, SCALES])
        neg_b3 = sb("neg_b3", [128, 1])
        ctx_exp = sb("ctx_exp", [128, TILES])
        ctx_den = sb("ctx_den", [128, TILES])
        ctx_sig = sb("ctx_sig", [128, TILES])
        ctx_w = sb("ctx_w", [128, TILES, SCALES])
        amps = sb("amps", [128, TILES, SCALES, D])
        hid1 = sb("hid1", [HID, BATCH, SEQ + K2 - 1])
        hid2 = amps[0:D, :, :, :].rearrange("p j s e -> p (j s e)")[:, 0:BATCH * (SEQ + K3 - 1)].rearrange(
            "p (b t) -> p b t", b=BATCH)
        xd = sb("xd", [128, RX, SEQ])
        nearest = sb("nearest", [128, SCALES, SEQ])
        turn = sb("turn", [128, RT, SCALES, SEQ])
        env = sb("env", [128, RE, SCALES, SEQ])

        h1 = sb("h1", [D, BATCH, SEQ])
        xn = sb("xn", [D, BATCH, SEQ + 2])
        y1n = ids_sb[0:D, :, :].bitcast(F32)

        s_first_in, s_const_in, s_ids_in = sem("s_first_in"), sem("s_const_in"), sem("s_ids_in")
        s_w128_in, s_w64_in, s_pos_in = sem("s_w128_in"), sem("s_w64_in"), sem("s_pos_in")
        s_hot = sem("s_hot")
        s_first = sem("s_first")
        s_firsthi = sem("s_firsthi")
        s_pad = sem("s_pad")
        s_gather = sem("s_gather")
        s_ampexp = sem("s_ampexp")
        s_param = sem("s_param")
        s_conv1 = sem("s_conv1")
        s_hid1 = sem("s_hid1")
        s_conv2 = sem("s_conv2")
        s_hid2 = sem("s_hid2")
        s_conv3 = sem("s_conv3")
        s_negb3 = sem("s_negb3")
        s_ctxexp = sem("s_ctxexp")
        s_amps = sem("s_amps")
        s_xd = sem("s_xd")
        s_square = sem("s_square")
        s_turned = sem("s_turned")
        s_turn = sem("s_turn")
        s_env = sem("s_env")
        s_sin = sem("s_sin")
        s_wave = sem("s_wave")
        s_last_wave = sem("s_last_wave")
        s_field = sem("s_field")
        s_h1 = sem("s_h1")
        s_dve = sem("s_dve")
        s_act = sem("s_act")
        s_fill = [sem("s_fill0"), sem("s_fill1")]
        s_evac = [sem("s_evac0"), sem("s_evac1")]

        def filled(eng, product, v):
            eng.wait_ge(s_fill[FILL[product, v] % 2], FILL[product, v] // 2 + 1)

        def evacuated(eng, product, v):
            eng.wait_ge(s_evac[FILL[product, v] % 2], FILL[product, v] // 2 + 1)

        names = ("rstd1 xn sp_arg sp_abs sp_parts dt dtx rest rest2 gate rstd2 sc2 y1n cgelu h1c rstd3 xn3 hx "
                 "rankbits out last_out bias column0 sel diag outwc").split()
        S = {n: sem("s_" + n) for n in names}
        s_stack = [sem(f"s_stack{g}") for g in range(G)]
        s_outdma = [sem("s_outdma0"), sem("s_outdma1")]
        s_dtrep = sem("s_dtrep")
        s_dxrep = sem("s_dxrep")
        s_decay = sem("s_decay")
        s_drive = sem("s_drive")
        s_state = sem("s_state")
        s_hc = sem("s_hc")
        s_ysum = sem("s_ysum")

        arena = [turn[:, i, :, :].rearrange("p s t -> p (s t)") for i in range(RT)]
        arena += [env[:, i, :, :].rearrange("p s t -> p (s t)") for i in range(RE)]

        def cut(i, rows=128):
            return arena[i][0:rows, :].rearrange("p (a t) -> p a t", t=SEQ)

        xi, sp2 = cut(RT + RE - 2)[:, 0:3], cut(RT + RE - 2)[:, 3:4]
        zs, gated = cut(RT + RE - 1)[:, 0:3], cut(RT + RE - 1)[:, 3:4]
        dt, dtx, rest = (cut(RT - 2)[:, i:i + n] for i, n in ((0, 1), (1, 1), (2, 2)))
        sp = cut(RT - 1)[:, 0:3]
        hot_f = hot[:, :, :].rearrange("p b t -> p (b t)").bitcast(F32)
        split_f = first_split[:, :, :].rearrange("p i n -> p (i n)").bitcast(F32)
        ln1_x, ln1_sq, ln1_r = hot_f[0:D, 0:SEQ], hot_f[0:D, SEQ:2 * SEQ], split_f[0:D, 0:SEQ]
        Bt, Ct = hid1[:, 0:2, 0:SEQ], hid1[:, 2:4, 0:SEQ]
        rest2 = first_rest[:, :, 0:SEQ]
        stack = amps[:, :, :, :].rearrange("p j s e -> p (j s e)").rearrange("p (q g t) -> p q g t", q=2, g=G)
        stack_hi = amps[:, :, :, :].rearrange("p j s e -> p (j s e)").bitcast(BF16).rearrange(
            "p (q g t w) -> p q g t w", q=2, g=G, w=2)[:, :, :, :, 1]
        hacc = cut(RT + RE - 3, D)
        ln_a, ln_b = (cut(RT + RE - 4, D)[:, 2 * i:2 * i + 2] for i in range(2))
        rows = [cut(i)[:, k, :] for i in (*range(RT - 2), *range(RT, RT + RE - 4)) for k in range(SCALES)]
        rows += [nearest[:, i, :] for i in range(SCALES)] + [xd[:, i, :] for i in range(RX)]
        decay, drive, state, hc = ([rows.pop(0) for _ in range(n)] for n in (RD, RC, RS, RH))
        wrow = pos_sb[:, 0:1, :]
        bits = [hot[:, t, 0:SEQ] for t in range(ST)]
        tie = sb("tie", [128, ST, 128], BF16)
        ones_bf = sb("ones_bf", [128, D], BF16)
        wcol = sb("wcol", [128, ST])
        ffh = pos_sb[:, 1:3, :]
        ffin = hacc[:, 0:2, :]
        mask = hacc[:, 2, :]
        sel_bf = sb("sel_bf", [128, PL, 128], BF16)
        out_wc = sb("out_wc", [128, D])
        out_wsum = sb("out_wsum", [128, 1])
        out_bc = sb("out_bc", [D, 1])
        diag = sb("diag", [D, KD, D])
        neg_A = sb("neg_A", [128, 2, P_DIM])
        dt_b = sb("dt_b", [128, 2])

        block = ctx.enter_context(nc.Block())

        @block.sync
        def _(sp_):
            sp_.dma_start(first, w128[:, 0:FIRST]).then_inc(s_first_in, 16)
            sp_.dma_start(const_sb[:, :], const).then_inc(s_const_in, 16)
            sp_.dma_start(ids_sb[:, :, :], ids).then_inc(s_ids_in, 16)
            sp_.dma_start(w128_sb[:, FIRST:], w128[:, FIRST:]).then_inc(s_w128_in, 16)
            sp_.dma_start(w64_sb[:, :], w64).then_inc(s_w64_in, 16)
            sp_.dma_start(pos_sb[:, :, :], pos).then_inc(s_pos_in, 16)
            sources = (cut(RT - 2)[:, 0:2], cut(RT - 2)[:, 2:4], rest2)
            sp_.wait_ge(s_field, TILES)
            for v in range(UNITS):
                sp_.wait_ge(S["rest2"], 2 * v + 2)
                for g in range(G):
                    if v >= 1:
                        sp_.wait_ge(s_dtrep, P_DIM * (v - 1) + PL * (g + 1))
                        sp_.wait_ge(s_dxrep, P_DIM * (v - 1) + PL * (g + 1))
                    for j, source in enumerate(sources):
                        sp_.dma_start(stack[32 * j:32 * j + 32, :, g, :], source[32 * g:32 * g + 32, :, :])\
                           .then_inc(s_stack[g], 16)
            for b in range(BATCH):
                if b < BATCH - 1:
                    sp_.wait_ge(S["out"], b + 1)
                else:
                    sp_.wait_ge(S["last_out"], 1)
                sp_.dma_start(out[:, b, :], ffin[:, b % 2, :]).then_inc(s_outdma[b % 2], 16)
            for i in range(2):
                sp_.wait_ge(s_outdma[i], 16 * BATCH // 2)

        @block.tensor
        def _(pe):
            mm = nc.tensor.matmul
            pe.wait_ge(s_first, 1)
            for j in range(TILES):
                b, t = divmod(j, ST)
                pe.wait_ge(s_hot, 2 * b + 2)
                for i in range(SPLITS):
                    last = mm(gathered[j // 6][:, (j % 6) * (D + 4):(j % 6 + 1) * (D + 4)],
                              hot[0:VOCAB, b, K1 // 2 + t * 128:K1 // 2 + (t + 1) * 128],
                              first_split[0:VOCAB, i, PAIRS * HID:], start=i == 0, stop=i == SPLITS - 1)
                last.then_inc(s_gather, 1)
            pe.wait_ge(s_pad, 1)

            def conv1(b):
                for k in range(PAIRS):
                    for i in range(SPLITS):
                        last = mm(conv_ps[b][:, :], first_split[:, i, k * HID:(k + 1) * HID], hot[:, b, 2 * k:2 * k + SEQ],
                                  start=k == 0 and i == 0, stop=k == PAIRS - 1 and i == SPLITS - 1)
                last.then_inc(s_conv1, 1)

            def conv2(b):
                pe.wait_ge(s_hid1, b + 1)
                for k in range(K2):
                    last = mm(conv_ps[b][0:D, :], tok_w2[:, k, :], hid1[:, b, k:k + SEQ], start=k == 0, stop=k == K2 - 1)
                last.then_inc(s_conv2, 1)

            def conv3(b):
                if b == 0:
                    pe.wait_ge(s_w64_in, 16)
                    pe.wait_ge(s_const_in, 16)
                    mm(ctx_logit[0:D, TILES:TILES + 1], centering, w64c("f_out_b"), start=True, stop=True)
                pe.wait_ge(s_hid2, b + 1)
                for t in range(ST):
                    for k in range(K3):
                        last = mm(ctx_logit[:, b * ST + t:b * ST + t + 1],
                                  hid2[:, b, t * 128 + k:t * 128 + k + 128], w64c("w3", k),
                                  start=k == 0, stop=k == K3 - 1)
                last.then_inc(s_conv3, 1)

            for conv in (conv1, conv2, conv3):
                for b in range(BATCH):
                    conv(b)

            def fill(product, v, rows, pairs):
                k = FILL[product, v]
                if k >= 2:
                    pe.wait_ge(s_evac[k % 2], k // 2)
                for i, (lhsT, rhs) in enumerate(pairs):
                    last = mm(shared[k % 2][0:rows, 0:rhs.shape[-1]], lhsT, rhs, start=i == 0, stop=i == len(pairs) - 1)
                last.then_inc(s_fill[k % 2], 1)

            def small(name, v):
                d, b = divmod(v, BATCH)
                D_ = "fb"[d]
                if name == "ln1_center":
                    pe.wait_ge(s_h1, b + 1)
                    fill("m1", v, D, [(centering, h1[:, b, :])])
                elif name == "conv":
                    pe.wait_ge(S["diag"], 1)
                    fill("cv", v, D, [(diag[:, k, :], xn[:, b, k:k + SEQ]) for k in range(KD)])
                elif name == "ln1_var":
                    evacuated(pe, "m1", v)
                    fill("v1", v, D, [(mean64, ln1_sq)])
                elif name in ("in_proj_x", "in_proj_z"):
                    if d == 0:
                        pe.wait_ge(S["xn"], b + 1)
                        x = xn[:, b, 1:SEQ + 1]
                    else:
                        pe.wait_ge(S["y1n"], b + 1)
                        x = y1n[:, b, :]
                    if name == "in_proj_x":
                        fill("xi", v, 128, [(w64c(D_ + "_in_wx"), x)])
                    else:
                        fill("z", v, 128, [(w64c(D_ + "_in_wz"), x)])
                elif name == "x_proj_dt":
                    evacuated(pe, "xi", v)
                    fill("dt", v, 128, [(w128c(D_ + "_xp_dt"), xi[:, v % 3, :])])
                elif name == "x_proj_B":
                    fill("B", v, 128, [(w128c(D_ + "_xp_B"), xi[:, v % 3, :])])
                elif name == "x_proj_C":
                    fill("C", v, 128, [(w128c(D_ + "_xp_C"), xi[:, v % 3, :])])
                elif name == "out_proj":
                    if v == 0:
                        pe.wait_ge(S["outwc"], 1)
                    pe.wait_ge(S["gate"], v + 1)
                    fill("o", v, D, [(w128c("b_out_w") if d else out_wc[:, :], gated[:, 0, :])])
                elif name == "ln2_var":
                    evacuated(pe, "o", v)
                    fill("v2", v, D, [(mean64, ln_b[:, 0, :])])
                elif name == "ln3_center":
                    evacuated(pe, "o", v)
                    fill("m3", v, D, [(centering, h1[:, b, :])])
                elif name == "ln3_var":
                    evacuated(pe, "m3", v)
                    fill("v3", v, D, [(mean64, ln_b[:, 0, :])])
                elif name == "ffn_route":
                    pe.wait_ge(S["xn3"], b + 1)
                    fill("w", v, 128, [(w64c("wr"), xn[:, b, 1:SEQ + 1])])
                elif name == "ffn_col":
                    evacuated(pe, "w", v)
                    k = FILL["wc", v]
                    pe.wait_ge(s_evac[k % 2], k // 2)
                    for t in range(ST):
                        last = nc.tensor.transpose(shared[k % 2][:, t:t + 1], wrow[0:1, 0, t * 128:(t + 1) * 128], constc("one")[0:1, :])
                    last.then_inc(s_fill[k % 2], 1)
                elif name == "ffn_rank_sum":
                    pe.wait_ge(S["rankbits"], ST * (b + 1))
                    k = FILL["rank", v]
                    pe.wait_ge(s_evac[k % 2], k // 2)
                    for t in range(ST):
                        mm(shared[k % 2][0:D, :], ones_bf[:, :], bits[t], start=t == 0, stop=False, skip_group_check=True)
                        last = mm(shared[k % 2][0:D, t * 128:(t + 1) * 128], ones_bf[:, :], tie[:, t, :], start=False,
                                  stop=t == ST - 1, skip_group_check=True)
                    last.then_inc(s_fill[k % 2], 1)
                elif name == "ffn_up":
                    for i in range(2):
                        fill(f"up{i}", v, 128, [(w64c("ffn_w1")[:, i * 128:(i + 1) * 128], xn[:, b, 1:SEQ + 1])])
                elif name == "ffn_down":
                    evacuated(pe, "up0", v)
                    evacuated(pe, "up1", v)
                    w2 = w128c("ffn_w2")
                    fill("y", v, D, [(w2[:, i * D:(i + 1) * D], ffh[:, i, :]) for i in range(2)])

            def replicate(q, c):
                v, p = divmod(c, P_DIM)
                g, l = divmod(p, PL)
                rep, made, used = ((dt_rep, s_dtrep, s_decay), (dx_rep, s_dxrep, s_drive))[q]
                if l == 0:
                    pe.wait_ge(s_stack[g], 16 * SPLITS * (v + 1))
                    if v == 0:
                        pe.wait_ge(S["sel"], g + 2)
                if c >= 2:
                    pe.wait_ge(used, c - 1)
                mm(rep[c % 2][:, :], sel_bf[:, l, :], stack_hi[:, q, g, :], start=True, stop=True).then_inc(made, 1)

            def sum_n(c):
                v, p = divmod(c, P_DIM)
                g, l = divmod(p, PL)
                if p == 0 and v >= 2:
                    pe.wait_ge(S["gate"], v - 1)
                pe.wait_ge(s_hc, c + 1)
                mm(y_ps[v % 2][32 * g:32 * g + 32, :], ssum[:, l, :], hc[c % RH], start=l == 0, stop=l == PL - 1,
                   tile_position=(0, 32 * g)).then_inc(s_ysum, 1)

            for j in range(TILES):
                b, t = divmod(j, ST)
                if t == 0:
                    pe.wait_ge(s_amps, b + 1)
                    if b >= 2:
                        pe.wait_ge(s_h1, b - 1)
                if j < TILES - 1:
                    pe.wait_ge(s_wave, j + 1)
                else:
                    pe.wait_ge(s_last_wave, 1)
                for s in range(SCALES):
                    last = mm(field_ps[b % 2][0:D, :], amps[:, j, s, :], env[:, j % RE, s, :],
                              start=t == 0 and s == 0, stop=t == ST - 1 and s == SCALES - 1)
                last.then_inc(s_field, 1)
                for name, v in early(SLOTS_PE.get(j, ())):
                    small(name, v)
            pe.wait_ge(s_h1, BATCH)

            for u, s in CORE_SLOTS:
                for name, v in PLAN.get((u, s), []):
                    small(name, v)
                if 0 <= u < UNITS:
                    c = u * P_DIM + s
                    if c == 0:
                        for k in range(LEAD_DT):
                            replicate(0, k)
                            if k < LEAD_DX:
                                replicate(1, k)
                    if c + LEAD_DT < UNITS * P_DIM:
                        replicate(0, c + LEAD_DT)
                    if c + LEAD_DX < UNITS * P_DIM:
                        replicate(1, c + LEAD_DX)
                    if c >= LAG:
                        sum_n(c - LAG)
                    if c == UNITS * P_DIM - 1:
                        for k in range(c - LAG + 1, c + 1):
                            sum_n(k)

        @block.vector
        def _(ve):
            v_ = nc.vector
            chain = [0]

            def link(ins):
                chain[0] += 1
                ins.then_inc(s_dve, 1)
                ve.wait_ge(s_dve, chain[0])

            half = K1 // 2
            v_.memset(hot[:, :, 0:half], 0.0)
            v_.memset(hot[:, :, SEQ + half - 1:SEQ + K1 - 1], 0.0)
            v_.memset(hid1[:, :, 0:2], 0.0)
            v_.memset(hid1[:, :, SEQ + 2:SEQ + 4], 0.0)
            v_.memset(hid2[:, :, 0:1], 0.0)
            v_.memset(hid2[:, :, SEQ + 1:SEQ + 2], 0.0)
            v_.memset(xn[:, :, 0:1], 0.0)
            v_.memset(ones_bf[:, :], 1.0)
            v_.memset(xn[:, :, SEQ + 1:SEQ + 2], 0.0).then_inc(s_pad, 1)
            ve.wait_ge(s_first_in, 16)
            ve.wait_ge(s_firsthi, 1)
            link(v_.tensor_tensor(first_rest[:, 0, :], first, first_split[:, 0, :], ALU.subtract))
            link(v_.tensor_copy(first_split[:, 1, :], first_rest[:, 0, :]))
            v_.tensor_tensor(first_split[:, 2, :], first_rest[:, 0, :], first_split[:, 1, :], ALU.subtract).then_inc(s_first, 1)
            ve.wait_ge(s_ids_in, 16)
            ve.wait_ge(s_const_in, 16)
            ve.wait_ge(s_pad, 1)
            for b in range(BATCH):
                for i in range(2):
                    rows = slice(VOCAB * i, VOCAB * i + VOCAB)
                    v_.tensor_scalar(hot[rows, b, half - i:half - i + SEQ], ids_sb[rows, b, :], constc("vocab")[rows, :], None,
                                     ALU.is_equal).then_inc(s_hot, 1)
            for k in range(3):
                n = min(6, TILES - 6 * k)
                ve.wait_ge(s_gather, 6 * k + n)
                last = v_.tensor_copy(loc[:, 6 * k:6 * k + n, :], gathered[k][:, 0:n * (D + 4)].rearrange("p (j e) -> p j e", j=n))
            link(last)
            ve.wait_ge(s_w128_in, 16)

            def over_scales(a):
                return a.unsqueeze(2).to_broadcast([128, TILES, SCALES])

            def over_tiles(a):
                return a.unsqueeze(1).to_broadcast([128, TILES, SCALES])

            lshift, lwidth, lamp, lphase = (loc[:, :, D + k] for k in range(4))
            v_.scalar_tensor_tensor(center[:, :], lshift, 0.05, constc("place"), ALU.mult, ALU.add)
            v_.tensor_scalar(phase[:, :], lphase, 0.5, 0.25, ALU.mult, ALU.add)
            link(v_.scalar_tensor_tensor(absw[:, :], lwidth, -1.0, lwidth, ALU.mult, ALU.max))
            link(v_.tensor_tensor(width[:, :, :], over_scales(absw[:, :]), over_tiles(w128c("widths")), ALU.mult))
            link(v_.tensor_scalar(width[:, :, :], width[:, :, :], 1e-5, None, ALU.add))
            link(v_.reciprocal(inv_w[:, :, :], width[:, :, :]))
            v_.scalar_tensor_tensor(neg_half[:, :, :], inv_w[:, :, :], -0.5, inv_w[:, :, :], ALU.mult, ALU.mult).then_inc(s_param, 1)

            def later_constants():
                v_.tensor_scalar(neg_b3[:, :], w128c("b3"), -1.0, None, ALU.mult).then_inc(s_negb3, 1)
                for d in range(2):
                    last = v_.tensor_tensor(dt_b[:, d:d + 1], w128c("fb"[d] + "_xp_bdt"), w128c("fb"[d] + "_dt_bias"), ALU.add)
                last.then_inc(S["bias"], 1)
                v_.memset(sel_bf[SPLITS * 32:128, :, :], 0.0)
                v_.tensor_copy(sel_bf[0:SPLITS * 32, :, :], sel[0:SPLITS * 32, :, :]).then_inc(S["sel"], 1)
                ve.wait_ge(s_w64_in, 16)
                link(v_.tensor_reduce(out_wsum[:, :], w128c("f_out_w"), mybir.AxisListType.X, ALU.add))
                link(v_.tensor_scalar(out_wsum[:, :], out_wsum[:, :], -1.0 / D, None, ALU.mult))
                v_.tensor_scalar(out_wc[:, :], w128c("f_out_w"), out_wsum[:, :], None, ALU.add).then_inc(S["outwc"], 1)
                for k in range(KD):
                    last = v_.tensor_scalar(diag[:, k, :], constc("eye")[0:D, :], w64c("conv_w", k), None, ALU.mult)
                last.then_inc(S["diag"], 1)

            def amplitudes():
                link(v_.tensor_tensor(sw2[:, :], w128c("sw"), w128c("sw"), ALU.mult))
                ve.wait_ge(s_ampexp, 1)
                link(v_.tensor_scalar(amp_den[:, :], amp_exp[:, :], 1.0, None, ALU.add))
                link(v_.reciprocal(amp_scale[:, :], amp_den[:, :]))
                link(v_.tensor_tensor(scale_w[:, :, :], over_scales(amp_scale[:, :]), over_tiles(sw2[:, :]), ALU.mult))
                ve.wait_ge(s_ctxexp, 1)
                link(v_.tensor_scalar(ctx_den[:, :], ctx_exp[:, :], 1.0, None, ALU.add))
                link(v_.reciprocal(ctx_sig[:, :], ctx_den[:, :]))
                link(v_.tensor_tensor(ctx_w[:, :, :], over_scales(ctx_sig[:, :]), scale_w[:, :, :], ALU.mult))
                for b in range(BATCH):
                    js = slice(b * ST, (b + 1) * ST)
                    v_.tensor_tensor(amps[:, js, :, :], loc[:, js, 0:D].unsqueeze(2).to_broadcast([128, ST, SCALES, D]),
                                     ctx_w[:, js, :].unsqueeze(3).to_broadcast([128, ST, SCALES, D]), ALU.mult).then_inc(s_amps, 1)

            def read(product, v):
                k = FILL[product, v]
                filled(ve, product, v)
                return shared[k % 2], s_evac[k % 2]

            def small(name, v):
                d, b = divmod(v, BATCH)
                D_ = "fb"[d]
                if name == "dt_log1p":
                    if v == 0:
                        ve.wait_ge(s_field, ST * (BATCH - 1))
                        ve.wait_ge(s_wave, ST * (BATCH - 1))
                    ve.wait_ge(S["sp_abs"], v + 1)
                    link(v_.tensor_scalar(sp2[:, 0, :], sp[:, 0, :], 1.0, -1.0, ALU.add, ALU.add))
                    link(v_.tensor_tensor(sp2[:, 0, :], sp2[:, 0, :], sp[:, 0, :], ALU.subtract))
                elif name == "dt_out":
                    ve.wait_ge(S["sp_parts"], v + 1)
                    if v:
                        ve.wait_ge(S["rest2"], 2 * v)
                        for g in range(G):
                            ve.wait_ge(s_stack[g], 16 * SPLITS * v)
                    link(v_.tensor_tensor(sp2[:, 0, :], sp[:, 2, :], sp2[:, 0, :], ALU.subtract))
                    v_.tensor_tensor(dt[:, 0, :], sp2[:, 0, :], sp[:, 1, :], ALU.add).then_inc(S["dt"], 1)
                elif name == "dtx_out":
                    ve.wait_ge(S["dt"], v + 1)
                    v_.tensor_tensor(dtx[:, 0, :], dt[:, 0, :], xi[:, v % 3, :], ALU.mult).then_inc(S["dtx"], 1)
                elif name == "gate":
                    if v:
                        filled(ve, "o", v - 1)
                    ve.wait_ge(s_ysum, P_DIM * (v + 1))
                    link(v_.scalar_tensor_tensor(gated[:, 0, :], xi[:, v % 3, :], w128c(D_ + "_D_skip"), y_ps[v % 2][:, :],
                                                 ALU.mult, ALU.add))
                    v_.tensor_tensor(gated[:, 0, :], gated[:, 0, :], zs[:, v % 3, :], ALU.mult).then_inc(S["gate"], 1)
                elif name == "ln2_scale":
                    ve.wait_ge(S["rstd2"], b + 1)
                    v_.scalar_tensor_tensor(ln_b[:, 0, :], ln_a[:, 0, :], w64c("norm_w"), ln_b[:, 1, :], ALU.mult, ALU.mult)\
                        .then_inc(S["sc2"], 1)
                elif name == "h2":
                    ps, ev = read("o", v)
                    ve.wait_ge(S["h1c"], b + 1)
                    v_.scalar_tensor_tensor(h1[:, b, :], ps[0:D, ::-1], w64c("b_out_b"), h1[:, b, :], ALU.add, ALU.add)\
                        .then_inc(ev, 1)
                elif name == "ln3_out":
                    ve.wait_ge(S["rstd3"], b + 1)
                    v_.tensor_tensor(xn[:, b, 1:SEQ + 1], ln_a[:, 1, :], ln_b[:, 1, :], ALU.mult).then_inc(S["xn3"], 1)
                elif name == "ffn_col_copy":
                    ps, ev = read("wc", v)
                    v_.tensor_copy(wcol[:, :], ps[:, 0:ST]).then_inc(ev, 1)
                elif name == "ffn_mask":
                    ps, ev = read("rank", v)
                    ve.wait_ge(S["h1c"], 3)
                    v_.scalar_tensor_tensor(mask[:, :], ps[0:D, :], CAP - 0.5, wrow[0:D, 0, :], ALU.is_lt, ALU.mult).then_inc(ev, 1)
                elif name[:-1] == "ffn_rank":
                    t = int(name[-1])
                    if t == 0:
                        evacuated(ve, "w", v)
                        evacuated(ve, "wc", v)
                    here = slice(t * 128, (t + 1) * 128)
                    v_.tensor_scalar(bits[t][:, 0:(t + 1) * 128], wrow[:, 0, 0:(t + 1) * 128], wcol[:, t:t + 1], None, ALU.is_lt)
                    if t + 1 < ST:
                        v_.tensor_scalar(bits[t][:, (t + 1) * 128:], wrow[:, 0, (t + 1) * 128:], wcol[:, t:t + 1], None, ALU.is_le)
                    last = v_.scalar_tensor_tensor(tie[:, t, :], wrow[:, 0, here], wcol[:, t:t + 1], constc("tri"),
                                                   ALU.is_equal, ALU.mult)
                    last.then_inc(S["rankbits"], 1)
                elif name == "ffn_out":
                    ps, ev = read("y", v)
                    if b >= 2:
                        ve.wait_ge(s_outdma[b % 2], 16 * (b // 2))
                    evacuated(ve, "rank", v)
                    v_.scalar_tensor_tensor(ffin[:, b % 2, :], ps[0:D, :], w64c("ffn_b2"), mask[:, :], ALU.add, ALU.mult)\
                        .then_inc(ev, 1)
                    if v == UNITS - 1:
                        evacuated(ve, "y", v)
                        ve.wait_ge(S["hx"], b + 1)
                        v_.tensor_tensor(ffin[:, b % 2, :], ffin[:, b % 2, :], h1[:, b, :], ALU.add).then_inc(S["last_out"], 1)

            def drive_step(c):
                v = c // P_DIM
                if c % P_DIM == 0:
                    evacuated(ve, "B", v)
                ve.wait_ge(s_dxrep, c + 1)
                v_.tensor_tensor(drive[c % RC], dx_rep[c % 2][:, :], Bt[:, v % 2, :], ALU.mult).then_inc(s_drive, 1)

            def scan_step(c):
                ve.wait_ge(s_decay, c + 1)
                ve.wait_ge(s_drive, c + 1)
                if c >= RS:
                    ve.wait_ge(s_hc, c - RS + 1)
                v_.tensor_tensor_scan(state[c % RS], decay[c % RD], drive[c % RC], 0.0,
                                      ALU.mult, ALU.add).then_inc(s_state, 1)

            ve.wait_ge(s_pos_in, 16)
            def distance(j):
                if j >= RX:
                    ve.wait_ge(s_env, j - RX + 1)
                v_.tensor_scalar(xd[:, j % RX, :], pos_sb[:, j // ST, :], center[:, j:j + 1], None, ALU.subtract).then_inc(s_xd, 1)

            for j in range(TILES):
                if j == 0:
                    distance(0)
                if j >= 1:
                    ve.wait_ge(s_turn, j)
                if j >= RT:
                    ve.wait_ge(s_wave, j - RT + 1)
                ve.wait_ge(s_xd, j + 1)
                for s in range(SCALES):
                    last = v_.tensor_scalar(turn[:, j % RT, s, :], xd[:, j % RX, :], inv_w[:, j, s:s + 1], phase[:, j:j + 1],
                                            ALU.mult, ALU.add)
                last.then_inc(s_turned, 1)
                if j + 1 < TILES:
                    distance(j + 1)
                ve.wait_ge(s_turned, j + 1)
                v_.tensor_tensor(xd[:, j % RX, :], xd[:, j % RX, :], xd[:, j % RX, :], ALU.mult).then_inc(s_square, 1)
                link(v_.tensor_scalar(nearest[:, :, :], turn[:, j % RT, :, :], ROUND, -ROUND, ALU.add, ALU.add))
                v_.tensor_tensor(turn[:, j % RT, :, :], turn[:, j % RT, :, :], nearest[:, :, :], ALU.subtract).then_inc(s_turn, 1)
                if j == 2:
                    later_constants()
                if j == AMPS_AT:
                    amplitudes()
                if j == TILES - 1:
                    ve.wait_ge(s_env, TILES)
                    ve.wait_ge(s_sin, TILES)
                    v_.tensor_tensor(env[:, j % RE, :, :], env[:, j % RE, :, :], turn[:, j % RT, :, :], ALU.mult)\
                        .then_inc(s_last_wave, 1)
                for name, v in early(SLOTS_DVE.get(j, ())):
                    small(name, v)
            ve.wait_ge(s_field, TILES)
            for tile in decay:
                last = v_.memset(tile[:, 0:1], 0.0)
            last.then_inc(S["column0"], 1)
            for g in range(G):
                v_.memset(stack[SPLITS * 32:128, :, g, :], 0.0).then_inc(S["sel"], 1)

            for u, s in CORE_SLOTS:
                for name, v in PLAN.get((u, s), []):
                    small(name, v)
                if 0 <= u < UNITS:
                    c = u * P_DIM + s
                    if c == 0:
                        for k in range(LEAD_DX):
                            drive_step(k)
                    if c + LEAD_DX < UNITS * P_DIM:
                        drive_step(c + LEAD_DX)
                    scan_step(c)

        @block.scalar
        def _(ac):
            act = nc.scalar.activation
            chain = [0]

            def link(ins):
                chain[0] += 1
                ins.then_inc(s_act, 1)
                ac.wait_ge(s_act, chain[0])

            ac.wait_ge(s_first_in, 16)
            act(first_split[:, 0, :], first, ACT.Copy).then_inc(s_firsthi, 1)
            ac.wait_ge(s_w128_in, 16)

            def hidden1(b):
                ac.wait_ge(s_conv1, b + 1)
                act(hid1[:, b, 2:2 + SEQ], conv_ps[b][:, :], ACT.Gelu, bias=w128c("tok_b1")).then_inc(s_hid1, 1)

            def hidden2(b):
                ac.wait_ge(s_conv2, b + 1)
                act(hid2[:, b, 1:1 + SEQ], conv_ps[b][0:D, :], ACT.Gelu, bias=w64c("b2")).then_inc(s_hid2, 1)

            def envelope(j):
                ac.wait_ge(s_square, j + 1)
                if j >= RE:
                    ac.wait_ge(s_field, j - RE + 1)
                for s in range(SCALES):
                    last = act(env[:, j % RE, s, :], xd[:, j % RX, :], ACT.Exp, scale=neg_half[:, j, s:s + 1])
                last.then_inc(s_env, 1)

            def wave(j):
                ac.wait_ge(s_turn, j + 1)
                act(turn[:, j % RT, :, :], turn[:, j % RT, :, :], ACT.Sin, scale=TWO_PI).then_inc(s_sin, 1)

            def field_out(b):
                ac.wait_ge(s_field, ST * (b + 1))
                act(h1[:, b, :], field_ps[b % 2][0:D, :], ACT.Copy).then_inc(s_h1, 1)

            def read(product, v):
                k = FILL[product, v]
                filled(ac, product, v)
                return shared[k % 2], s_evac[k % 2]

            def rstd(product, v, out_):
                ps, ev = read(product, v)
                act(out_, ps[0:D, :], ACT.Ln, bias=constc("eps")[0:D, :]).then_inc(ev, 1)
                evacuated(ac, product, v)

            def small(name, v):
                d, b = divmod(v, BATCH)
                D_ = "fb"[d]
                if name == "ln1_square":
                    ps, ev = read("m1", v)
                    if b:
                        ac.wait_ge(S["xn"], b)
                    act(ln1_x, ps[0:D, :], ACT.Copy)
                    act(ln1_sq, ps[0:D, :], ACT.Square).then_inc(ev, 1)
                elif name == "ln1_rstd":
                    rstd("v1", v, ln1_r)
                    act(ln1_r, ln1_r, ACT.Exp, scale=-0.5).then_inc(S["rstd1"], 1)
                elif name == "silu":
                    if v == 0:
                        ac.wait_ge(s_field, ST * (BATCH - 1))
                    if v >= 3:
                        ac.wait_ge(S["gate"], v - 2)
                    for product, bias, to in (("xi", "_in_bx", xi), ("z", "_in_bz", zs)):
                        ps, ev = read(product, v)
                        act(to[:, v % 3, :], ps[:, :], ACT.Silu, bias=w128c(D_ + bias)).then_inc(ev, 1)
                    nc.scalar.preload_act_table_set("natural_log_exp_and_others")
                elif name == "softplus_arg":
                    ps, ev = read("dt", v)
                    if v == 0:
                        ac.wait_ge(s_wave, ST * (BATCH - 1))
                    if v:
                        ac.wait_ge(S["dt"], v)
                    act(sp[:, 0, :], ps[:, :], ACT.Abs, bias=dt_b[:, d:d + 1]).then_inc(S["sp_arg"], 1)
                    act(sp[:, 1, :], ps[:, :], ACT.Relu, bias=dt_b[:, d:d + 1]).then_inc(ev, 1)
                elif name == "softplus_log":
                    ac.wait_ge(S["sp_arg"], v + 1)
                    act(sp[:, 0, :], sp[:, 0, :], ACT.Exp, scale=-1.0).then_inc(S["sp_abs"], 1)
                    ac.wait_ge(S["sp_abs"], v + 1)
                    act(sp[:, 2, :], sp[:, 0, :], ACT.Ln, bias=constc("one")).then_inc(S["sp_parts"], 1)
                    ps, ev = read("B", v)
                    if v >= 2:
                        ac.wait_ge(s_drive, P_DIM * (v - 1))
                    act(Bt[:, v % 2, :], ps[:, :], ACT.Identity, bias=w128c(D_ + "_xp_bB")).then_inc(ev, 1)
                elif name == "C_out":
                    ps, ev = read("C", v)
                    if v >= 2:
                        ac.wait_ge(s_hc, P_DIM * (v - 1))
                    act(Ct[:, v % 2, :], ps[:, :], ACT.Identity, bias=w128c(D_ + "_xp_bC")).then_inc(ev, 1)
                elif name == "conv_out":
                    ps, ev = read("cv", v)
                    act(hacc[:, b, :], ps[0:D, :], ACT.Copy).then_inc(ev, 1)
                elif name == "ln2_square":
                    ps, ev = read("o", v)
                    if b:
                        ac.wait_ge(S["sc2"], b)
                    act(ln_a[:, 0, :], ps[0:D, :], ACT.Identity, bias=out_bc[:, :])
                    act(ln_b[:, 0, :], ps[0:D, :], ACT.Square, bias=out_bc[:, :]).then_inc(ev, 1)
                elif name == "ln2_rstd":
                    rstd("v2", v, ln_b[:, 1, :])
                    act(ln_b[:, 1, :], ln_b[:, 1, :], ACT.Exp, scale=-0.5).then_inc(S["rstd2"], 1)
                elif name == "ln2_out":
                    ac.wait_ge(S["sc2"], b + 1)
                    act(y1n[:, b, ::-1], ln_b[:, 0, :], ACT.Identity, bias=w64c("norm_b")).then_inc(S["y1n"], 1)
                elif name == "ln3_square":
                    ps, ev = read("m3", v)
                    if b:
                        ac.wait_ge(S["xn3"], b)
                    act(ln_a[:, 1, :], ps[0:D, :], ACT.Copy)
                    act(ln_b[:, 0, :], ps[0:D, :], ACT.Square).then_inc(ev, 1)
                elif name == "ln3_rstd":
                    if b:
                        ac.wait_ge(S["xn3"], b)
                    rstd("v3", v, ln_b[:, 1, :])
                    act(ln_b[:, 1, :], ln_b[:, 1, :], ACT.Exp, scale=-0.5).then_inc(S["rstd3"], 1)
                elif name == "ffn_route_copy":
                    ps, ev = read("w", v)
                    if b:
                        evacuated(ac, "rank", v - 1)
                    act(wrow[:, 0, :], ps[:, :], ACT.Identity, bias=w128c("br")).then_inc(ev, 1)
                elif name == "conv_gelu":
                    evacuated(ac, "cv", BATCH - 1)
                    act(hacc[:, :, :], hacc[:, :, :], ACT.Gelu, bias=w64c("conv_b")).then_inc(S["cgelu"], 1)
                    nc.scalar.preload_act_table_set("natural_log_exp_and_others")
                elif name == "ffn_gelu":
                    if b:
                        filled(ac, "y", v - 1)
                    for i in range(2):
                        ps, ev = read(f"up{i}", v)
                        act(ffh[:, i, :], ps[:, :], ACT.Gelu_apprx_tanh, bias=w128c("ffn_b1", i)).then_inc(ev, 1)
                    nc.scalar.preload_act_table_set("natural_log_exp_and_others")

            def decay_step(c):
                d, p = c // P_DIM // BATCH, c % P_DIM
                ac.wait_ge(s_dtrep, c + 1)
                if c >= RD:
                    ac.wait_ge(s_state, c - RD + 1)
                act(decay[c % RD][:, 1:], dt_rep[c % 2][:, 1:], ACT.Exp, scale=neg_A[:, d, p:p + 1]).then_inc(s_decay, 1)

            def context(_):
                ac.wait_ge(s_conv3, BATCH)
                ac.wait_ge(s_negb3, 1)
                act(ctx_exp[:, :], ctx_logit[:, 0:TILES], ACT.Exp, bias=neg_b3[:, :], scale=-1.0).then_inc(s_ctxexp, 1)
                act(out_bc[:, :], ctx_logit[0:D, TILES:TILES + 1], ACT.Copy)
                for d in range(2):
                    last = act(neg_A[:, d, :], w128c("fb"[d] + "_A_log"), ACT.Exp)
                link(last)
                link(act(neg_A[:, :, :], neg_A[:, :, :], ACT.Copy, scale=-1.0))

            def amp_exponent(_):
                ac.wait_ge(s_param, 1)
                act(amp_exp[:, :], loc[:, :, D + 2], ACT.Exp, scale=-1.0).then_inc(s_ampexp, 1)

            def slot(s):
                for name, v in early([s]):
                    small(name, v)

            ac.wait_ge(s_w64_in, 16)
            jobs = {"hidden1": hidden1, "hidden2": hidden2, "envelope": envelope, "wave": wave, "context": context, "amp_exponent": amp_exponent,
                    "field_out": field_out, "slot": slot}
            for kind, t in TOKEN_ORDER:
                jobs[kind](t)
            ac.wait_ge(S["column0"], 1)
            ac.wait_ge(S["bias"], 1)

            for u, s in CORE_SLOTS:
                for name, v in PLAN.get((u, s), []):
                    small(name, v)
                if 0 <= u < UNITS:
                    c = u * P_DIM + s
                    if c == 0:
                        for k in range(LEAD_DECAY):
                            decay_step(k)
                    if c + LEAD_DECAY < UNITS * P_DIM:
                        decay_step(c + LEAD_DECAY)

        @block.gpsimd
        def _(po):
            tt = nc.gpsimd.tensor_tensor
            def small(name, v):
                d, b = divmod(v, BATCH)
                if name == "ln1_out":
                    po.wait_ge(S["rstd1"], b + 1)
                    tt(xn[:, b, 1:SEQ + 1], ln1_x, ln1_r, ALU.mult).then_inc(S["xn"], 1)
                elif name in ("dt_parts", "dtx_parts"):
                    q = int(name == "dtx_parts")
                    po.wait_ge(S["dtx" if q else "dt"], v + 1)
                    upper = cut(RT - 2)[:, q, :].bitcast(BF16).rearrange("p (t w) -> p t w", w=2)[:, :, 1]
                    tt(rest[:, q, :], cut(RT - 2)[:, q, :], upper, ALU.subtract).then_inc(S["rest"], 1)
                    po.wait_ge(S["rest"], 2 * v + q + 1)
                    upper = rest[:, q, :].bitcast(BF16).rearrange("p (t w) -> p t w", w=2)[:, :, 1]
                    tt(rest2[:, q, :], rest[:, q, :], upper, ALU.subtract).then_inc(S["rest2"], 1)
                elif name == "conv_add":
                    po.wait_ge(S["cgelu"], 1)
                    tt(h1[:, v, :], h1[:, v, :], hacc[:, v, :], ALU.add).then_inc(S["h1c"], 1)
                elif name == "residual":
                    po.wait_ge(S["xn3"], b + 1)
                    tt(h1[:, b, :], h1[:, b, :], xn[:, b, 1:SEQ + 1], ALU.add).then_inc(S["hx"], 1)
                elif name == "ffn_out" and v < UNITS - 1:
                    evacuated(po, "y", v)
                    po.wait_ge(S["hx"], b + 1)
                    tt(ffin[:, b % 2, :], ffin[:, b % 2, :], h1[:, b, :], ALU.add).then_inc(S["out"], 1)

            def read_out(c):
                v = c // P_DIM
                if c % P_DIM == 0:
                    evacuated(po, "C", v)
                po.wait_ge(s_state, c + 1)
                if c >= RH:
                    po.wait_ge(s_ysum, c - RH + 1)
                tt(hc[c % RH], state[c % RS], Ct[:, v % 2, :], ALU.mult).then_inc(s_hc, 1)

            for j in range(TILES - 1):
                po.wait_ge(s_env, j + 1)
                po.wait_ge(s_sin, j + 1)
                tt(env[:, j % RE, :, :], env[:, j % RE, :, :], turn[:, j % RT, :, :], ALU.mult).then_inc(s_wave, 1)
                for name, v in early(SLOTS_POOL.get(j, ())):
                    small(name, v)

            for u, s in CORE_SLOTS:
                for name, v in PLAN.get((u, s), []):
                    small(name, v)
                if 0 <= u < UNITS:
                    read_out(u * P_DIM + s)


def constants():
    c = {}
    r = np.arange(128)
    h_r, l_r = r % 32 // PL, r % PL
    c["sel"] = ((l_r[:, None, None] == np.arange(PL)[None, :, None])
                & (h_r[:, None, None] == (r // N_DIM)[None, None, :])).reshape(128, -1)
    q = np.arange(32)
    c["ssum"] = (((r // N_DIM)[:, None, None] == (q // PL)[None, None, :])
                 & (np.arange(PL)[None, :, None] == (q % PL)[None, None, :])).reshape(128, -1)
    c["tri"] = r[:, None] < r[None, :]
    line = (np.arange(SEQ, dtype=np.float32) / np.float32(SEQ - 1)).astype(np.float32)
    c["place"] = np.tile(line.reshape(ST, 128).T, (1, BATCH))
    c["eps"] = np.full((128, 1), LN_EPS)
    c["one"] = np.ones((128, 1))
    c["mean"] = np.full((128, D), 1.0 / D)
    c["centering"] = np.eye(128, D) - 1.0 / D
    c["eye"] = np.eye(128, D)
    c["vocab"] = r[:, None] % VOCAB
    out = np.zeros((128, C128_N), np.float32)
    for name, (a, b) in C128.items():
        out[:, a:b] = c[name]
    return out


def kernel(**inputs):
    import concourse.bacc as bacc
    from concourse.bass_utils import run_bass_kernel_spmd

    x = {k: np.asarray(v) for k, v in inputs.items()}
    perm = np.arange(DI).reshape(HEADS, G, PL).transpose(1, 0, 2).reshape(-1)

    def row(a, p=128):
        return np.broadcast_to(a.reshape(1, -1), (p, a.size))

    w1 = np.zeros((2, VOCAB, PAIRS, HID), np.float32)
    for k in range(K1):
        w1[k % 2, :, k // 2, :] = x["L0_tok_w1"][:, :, k].T
    embloc = np.zeros((128, D + 4), np.float32)
    embloc[:VOCAB] = np.concatenate([x["L0_tok_emb"], x["L0_tok_locality_shapes"]], 1)
    p128 = {
        "tok_w1": w1.reshape(128, -1), "embloc": embloc,
        "tok_w2": x["L0_tok_w2"].transpose(1, 2, 0).reshape(HID, -1), "tok_b1": x["L0_tok_b1"][:, None],
        "b3": row(x["L0_tok_b3"]), "widths": row(x["L0_tok_multiscale_widths"]), "sw": row(x["L0_tok_scale_weights"]),
        "br": row(x["L0_ffn_br"]),
        "ffn_w2": x["L0_ffn_w2"].reshape(2, 128, D).transpose(1, 0, 2).reshape(128, -1),
        "ffn_b1": x["L0_ffn_b1"].reshape(2, 128).T,
    }
    p64 = {
        "w3": x["L0_tok_w3"][0], "b2": x["L0_tok_b2"][:, None],
        "norm_w": x["L0_attn_norm_w"][:, None], "norm_b": x["L0_attn_norm_b"][:, None],
        "conv_w": x["L0_attn_conv_w"][:, 0, :], "conv_b": x["L0_attn_conv_b"][:, None],
        "ffn_w1": x["L0_ffn_w1"], "wr": np.broadcast_to(x["L0_ffn_wr"], (D, 128)), "ffn_b2": x["L0_ffn_b2"][:, None],
    }
    for d in "fb":
        g = {k[len("L0_attn_f_"):]: v for k, v in x.items() if k.startswith(f"L0_attn_{d}_")}
        xp, xb = g["x_proj_w"][:, perm], g["x_proj_b"][:, None]
        p128 |= {
            f"{d}_xp_dt": xp[:DI][perm].T, f"{d}_xp_B": xp[DI:2 * DI].T, f"{d}_xp_C": xp[2 * DI:].T,
            f"{d}_in_bx": g["in_proj_b"][:DI][perm][:, None], f"{d}_in_bz": g["in_proj_b"][DI:][perm][:, None],
            f"{d}_xp_bdt": xb[:DI][perm], f"{d}_dt_bias": g["dt_bias"][perm][:, None],
            f"{d}_xp_bB": xb[DI:2 * DI], f"{d}_xp_bC": xb[2 * DI:], f"{d}_D_skip": g["D_skip"][perm][:, None],
            f"{d}_A_log": g["A_log"].reshape(HEADS, P_DIM, N_DIM).transpose(0, 2, 1).reshape(128, P_DIM),
            f"{d}_out_w": g["out_proj_w"][:, perm].T,
        }
        p64 |= {f"{d}_in_wx": g["in_proj_w"][:DI][perm].T, f"{d}_in_wz": g["in_proj_w"][DI:][perm].T,
                f"{d}_out_b": g["out_proj_b"][:, None]}

    def side_by_side(parts, places):
        return np.ascontiguousarray(np.concatenate([parts[n] for n in places], 1))

    arrays = {
        "ids": np.ascontiguousarray(np.broadcast_to(x["x"], (128, BATCH, SEQ))),
        "w64": side_by_side(p64, W64), "w128": side_by_side(p128, W128),
        "pos": np.ascontiguousarray(np.broadcast_to(x["fside_BS_continuous_positions"], (128, BATCH, SEQ))),
        "const": constants(),
    }
    nc = bacc.Bacc("TRN2", target_bir_lowering=False, num_devices=1)
    args = [nc.dram_tensor(n, a.shape, mybir.dt.from_np(a.dtype), kind="ExternalInput").ap() for n, a in arrays.items()]
    out = nc.dram_tensor("out", (D, BATCH, SEQ), F32, kind="ExternalOutput").ap()
    build(nc, *args, out)
    r = run_bass_kernel_spmd(nc, [arrays], core_ids=[0])
    return r.results[0]["out"].transpose(1, 2, 0)
```
